# Optimizing a Trainium2 kernel written in Bass

```python
import numpy as np
import jax
import jax.numpy as jnp

def _softmax(x, axis=-1):
    return jax.nn.softmax(x, axis=axis)

def _gelu(x):
    return jax.nn.gelu(x, approximate=True)

def _silu(x):
    return jax.nn.silu(x)

def _sigmoid(x):
    return jax.nn.sigmoid(x)

def _layernorm(x, axis=-1, eps=1e-05):
    m = jnp.mean(x, axis=axis, keepdims=True)
    v = jnp.var(x, axis=axis, keepdims=True)
    return (x - m) / jnp.sqrt(v + eps)

def _scatter_add(tgt, idx, src, axis=0):
    return tgt.at[idx].add(src)

def _segment_sum(src, seg, n):
    return jax.ops.segment_sum(src, seg, n)
kernel_name = 'mk_prb_d1_jaxref_r8_747e66'

def setup_inputs(seed: int=0):
    np.random.seed(seed)
    _w = jnp.asarray

    def _L0_attn_setup():
        import jax, jax.numpy as jnp
        import numpy as np
        D_MODEL = 128
        NUM_HEADS = 16
        D_K = D_MODEL // NUM_HEADS
        BATCH, SEQ = (2, 256)
        key = jax.random.key(seed)
        k = jax.random.split(key, 5)
        std = np.sqrt(2.0 / (D_MODEL + D_MODEL)).astype(np.float32)
        return {'x': jax.random.normal(k[0], (BATCH, SEQ, D_MODEL), dtype=jnp.float32), 'WQ': jax.random.normal(k[1], (D_MODEL, D_MODEL), dtype=jnp.float32) * std, 'WK': jax.random.normal(k[2], (D_MODEL, D_MODEL), dtype=jnp.float32) * std, 'WV': jax.random.normal(k[3], (D_MODEL, D_MODEL), dtype=jnp.float32) * std, 'WO': jax.random.normal(k[4], (D_MODEL, D_MODEL), dtype=jnp.float32) * std}
    _L0_attn_in = _L0_attn_setup()

    def _L0_ffn_setup():
        import jax, jax.numpy as jnp
        import numpy as np
        FEATURES = 128
        D_IN = 128

        def fp8_gemm_optimized(x, input_scale, kernel, kernel_scale):
            s_in = input_scale[0]
            s_k = kernel_scale[0]
            x_q = (x.astype(jnp.float32) / s_in).astype(jnp.float8_e4m3fn)
            k_q = (kernel.astype(jnp.float32) / s_k).astype(jnp.float8_e4m3fn)
            y = jnp.dot(x_q.astype(jnp.float32), k_q.astype(jnp.float32), preferred_element_type=jnp.float32)
            return y * (s_in * s_k)
        key = jax.random.key(seed)
        kx, kk, kb = jax.random.split(key, 3)
        x = jax.random.normal(kx, (4, 1024, D_IN), dtype=jnp.float32)
        limit = np.sqrt(6.0 / (D_IN + FEATURES)).astype(np.float32)
        kernel = jax.random.uniform(kk, (D_IN, FEATURES), dtype=jnp.float32, minval=-limit, maxval=limit).astype(jnp.bfloat16)
        input_scale = jnp.ones((1,), dtype=jnp.float32)
        kernel_scale = jnp.ones((1,), dtype=jnp.float32)
        bias = jnp.zeros((FEATURES,), dtype=jnp.bfloat16)
        return {'x': x, 'kernel': kernel, 'input_scale': input_scale, 'kernel_scale': kernel_scale, 'bias': bias}
    _L0_ffn_in = _L0_ffn_setup()
    _d = {'L0_attn_x': _L0_attn_in['x'], 'L0_attn_WQ': _L0_attn_in['WQ'], 'L0_attn_WK': _L0_attn_in['WK'], 'L0_attn_WV': _L0_attn_in['WV'], 'L0_attn_WO': _L0_attn_in['WO'], 'L0_ffn_kernel': _L0_ffn_in['kernel'], 'L0_ffn_input_scale': _L0_ffn_in['input_scale'], 'L0_ffn_kernel_scale': _L0_ffn_in['kernel_scale'], 'L0_ffn_bias': _L0_ffn_in['bias']}
    _x0 = _d['L0_attn_x']
    _d['L0_attn_x'] = jax.random.normal(jax.random.fold_in(jax.random.key(seed), 1), (2, 1024, 128), dtype=_x0.dtype)
    del _x0
    return _d

def reference(L0_attn_x, L0_attn_WQ, L0_attn_WK, L0_attn_WV, L0_attn_WO, L0_ffn_kernel, L0_ffn_input_scale, L0_ffn_kernel_scale, L0_ffn_bias):

    def _L0_attn_ref(x, WQ, WK, WV, WO):
        import jax, jax.numpy as jnp
        import numpy as np
        D_MODEL = 128
        NUM_HEADS = 16
        D_K = D_MODEL // NUM_HEADS
        BATCH, SEQ = (2, 256)
        B, S, E = x.shape
        mask = jnp.where(jnp.triu(jnp.ones((S, S), dtype=bool), k=1), -jnp.inf, 0.0).astype(x.dtype)

        def heads(W):
            return (x @ W).reshape(B, S, NUM_HEADS, D_K).transpose(0, 2, 1, 3)
        Q, K, V = (heads(WQ), heads(WK), heads(WV))
        score = jnp.einsum('bhqd,bhkd->bhqk', Q, K) / jnp.sqrt(jnp.asarray(D_K, x.dtype))
        score = score + mask
        score = score - jnp.max(score, axis=-1, keepdims=True)
        score = jnp.exp(score)
        score = score / jnp.sum(score, axis=-1, keepdims=True)
        out = jnp.einsum('bhqk,bhkd->bhqd', score, V)
        out = out.transpose(0, 2, 1, 3).reshape(B, S, E)
        return out @ WO

    def _L0_ffn_ref(x, kernel, input_scale, kernel_scale, bias):
        import jax, jax.numpy as jnp
        import numpy as np
        FEATURES = 128
        D_IN = 128

        def fp8_gemm_optimized(x, input_scale, kernel, kernel_scale):
            s_in = input_scale[0]
            s_k = kernel_scale[0]
            x_q = (x.astype(jnp.float32) / s_in).astype(jnp.float8_e4m3fn)
            k_q = (kernel.astype(jnp.float32) / s_k).astype(jnp.float8_e4m3fn)
            y = jnp.dot(x_q.astype(jnp.float32), k_q.astype(jnp.float32), preferred_element_type=jnp.float32)
            return y * (s_in * s_k)
        dtype = jnp.bfloat16
        x = x.astype(dtype)
        orig_shape = x.shape
        x2 = x.reshape(-1, x.shape[-1])
        y = fp8_gemm_optimized(x2, input_scale, kernel, kernel_scale)
        y = y.astype(dtype) + bias
        return y.reshape(orig_shape[:-1] + (FEATURES,))
    x = L0_attn_x
    xn = _layernorm(x, axis=-1)
    x = x + _L0_attn_ref(xn, L0_attn_WQ, L0_attn_WK, L0_attn_WV, L0_attn_WO) + _L0_ffn_ref(xn, L0_ffn_kernel, L0_ffn_input_scale, L0_ffn_kernel_scale, L0_ffn_bias)
    return x

_drawn_inputs = setup_inputs


def setup_inputs(seed=0):
    import zlib

    import numpy as np

    out = dict(_drawn_inputs(seed))
    spreads = {'L0_ffn_bias': (0.0, 0.1)}
    factors = {}
    for name, (base, spread) in spreads.items():
        noise = np.random.default_rng([zlib.crc32(name.encode()), seed]).standard_normal(out[name].shape)
        drawn = base * np.exp(spread * noise) if base else spread * noise
        out[name] = jnp.asarray(drawn.astype(out[name].dtype))
    for name, factor in factors.items():
        out[name] = (out[name] * factor).astype(out[name].dtype)
    return out
```

```python
import concourse.bass as bass
from concourse import mybir
from contextlib import ExitStack

fp32 = mybir.dt.float32
bf16 = mybir.dt.bfloat16
fp8 = mybir.dt.float8e4
u32 = mybir.dt.uint32
ALU = mybir.AluOpType
ACT = mybir.ActivationFunctionType
AX = mybir.AxisListType

B, S, D = 2, 1024, 128
H = 16
DK = D // H
J = 4
GB = H // J
NG = B * GB
T = S // 128
C = 512
NC = S // C
TC = C // 128
NP = 3
SPLIT_ROWS = NP * NP * DK
PAD_ROWS = 96
MAX_ROWS = PAD_ROWS + NP
VW = 32
MASKED = -3.0e38
EPS = 1e-5
SCALE = float(DK) ** -0.5
BF16_ONES = 1.0019378662109375
FP8_TOP = 240.0
OVERFLOW = 7.3e35
P_RING = 6
S_RING = 2
A_RING = 3


def score_steps():
    steps = []
    for c in range(NC):
        first = TC * c
        for kb in range(first + 1):
            for pair in range(2):
                steps.append((c, [(C * n, 2 * pair + n, kb, 0, C, kb == first) for n in range(2)]))
        for pair in range(2):
            steps.append((c, [p for n in range(2) for p in (
                (C * n, 2 * pair + n, first + 1, 128, 384, True),
                (C * n + 384, 2 * pair + n, first + 3, 384, 128, True))]))
        steps.append((c, [(256 * j, j, first + 2, 256, 256, True) for j in range(J)]))
    return steps


def max_units():
    units = []
    for pair in (0, 2):
        for j in (pair, pair + 1):
            units.append((0, [(0, j, 3, 0, 4, True)], [(0, 1, 512, j, 3, None)]))
        for j in (pair, pair + 1):
            units.append((0, [(0, j, 2, 0, 3, True), (384, j, 0, 0, 1, True)],
                          [(0, 1, 384, j, 2, None), (384, 1, 128, j, 0, None)]))
        units.append((0, [(0, pair, 1, 0, 2, True), (256, pair + 1, 1, 0, 2, True)],
                      [(0, 2, 256, pair, 1, None)]))
    for pair in (0, 2):
        for j in (pair, pair + 1):
            for i in range(4, 8):
                units.append((1, [(0, j, i, 0, 4, False)], [(0, 1, 512, j, i, 0)]))
            units.append((1, [(0, j, 7, 4, 4, True)], [(0, 1, 512, j, 7, 1)]))
            units.append((1, [(0, j, 6, 4, 3, True), (384, j, 4, 4, 1, True)],
                          [(0, 1, 384, j, 6, 1), (384, 1, 128, j, 4, 1)]))
        units.append((1, [(0, pair, 5, 4, 2, True), (256, pair + 1, 5, 4, 2, True)],
                      [(0, 2, 256, pair, 5, 1)]))
    return units


STEPS = score_steps()
NSTEP = len(STEPS)
UNITS = max_units()
N0 = sum(c == 0 for c, _, _ in UNITS)
TURN = "turn"
RING = UNITS[:N0 + 4] + [(TURN, 0)] + [*UNITS[N0 + 4:], (TURN, 1)]
RING_ADD = -len(RING) % A_RING
NR = len(RING) + RING_ADD
Q0_FREE = sum(c == 0 for c, _ in STEPS)
K0_FREE = Q0_FREE + 2 * TC
VALUES = {}
_s = 0
while _s < NSTEP:
    _n = 1 if _s + 1 == NSTEP or STEPS[_s + 1][0] != STEPS[_s][0] else 2
    VALUES[_s + _n - 1 + 2] = list(range(_s, _s + _n))
    _s += _n
O0_DONE = Q0_FREE - 1 + 2
LAST_PLACE = NSTEP + 1
PLACES = {}
for _n in range(len(RING) - 1):
    PLACES.setdefault(2 + _n * (LAST_PLACE - 2) // (len(RING) - 1), []).append(_n)
PLACES.setdefault(LAST_PLACE, []).append(len(RING) - 1)


def attention_kernel(nc, x, wq, wk, wv, wo, wf, s_in, s_k, bias, out):
    ctx = ExitStack()
    with ctx:
        def sb(name, shape, dt):
            return ctx.enter_context(nc.sbuf_tensor(name, shape, dt))

        def sem(name):
            return ctx.enter_context(nc.semaphore(name))

        parts_dram = nc.dram_tensor("parts_dram", (2, NC, NG, DK, NP, J, C), bf16, kind="Internal").ap()
        raw_dram = nc.dram_tensor("raw_dram", (NG, 128, S), fp32, kind="Internal").ap()

        xs = sb("xs", [128, B * T, D], fp32)
        xn = sb("xn", [128, B * T, D], fp32)
        stats = sb("stats", [128, B * T, 6], fp32)
        moments = sb("moments", [128, B * T, 2], fp32)
        std = sb("std", [128, B * T], fp32)
        rstd = sb("rstd", [128, B * T], fp32)
        eps = sb("eps", [128, 1], fp32)
        w_sb = sb("w_sb", [128, 4, D], fp32)
        w_qk = sb("w_qk", [128, 2, D], fp32)
        wf_sb = sb("wf_sb", [128, D], bf16)
        bias_sb = sb("bias_sb", [128, D], bf16)
        scales = sb("scales", [128, 2], fp32)
        inverse = sb("inverse", [128, 2], fp32)
        half_inverse = sb("half_inverse", [128, 2], fp32)
        scale_both = sb("scale_both", [128, 1], fp32)
        identf = sb("identf", [128, 128], fp32)
        identb = sb("identb", [128, 128], bf16)
        mask_qk = sb("mask_qk", [128, 128], bf16)
        mask_kq = sb("mask_kq", [128, 128], bf16)
        xnT = sb("xnT", [128, B * S], fp32)
        xnTb = sb("xnTb", [128, B * S], bf16)
        parts = sb("parts", [128, 2, NP, B * S], bf16)
        rest = sb("rest", [128, 2, C], fp32)
        qk1 = sb("qk1", [128, 2, S], fp32)
        v_all = sb("v_all", [128, NG, T, 32], fp32)
        xq = sb("xq", [128, B * S], bf16)
        kq = sb("kq", [128, D], bf16)
        f_a = sb("f_a", [128, C], fp32)
        f_b = sb("f_b", [128, C], fp32)
        f_c = sb("f_c", [128, C], fp32)
        f8_big = sb("f8_big", [128, C], fp8)
        f8_small = sb("f8_small", [128, C], fp8)

        qr = sb("qr", [128, 2, NC, J, C], bf16)
        kr = sb("kr", [128, 2, NC, J, C], bf16)
        vr = sb("vr", [128, 2, T, J, VW], fp32)
        probs = sb("probs", [128, P_RING, 2 * C], fp32)
        part_max = sb("part_max", [128, J * TC, 2], fp32)
        neg_max = sb("neg_max", [128, NC, J * TC], fp32)
        max_rest = sb("max_rest", [J * TC, 128], fp32)
        max_parts = sb("max_parts", [J * TC, NC, NP, 128], bf16)
        raw_sb = sb("raw_sb", [128, NC, C], fp32)
        att = sb("att", [128, NC * B, C], fp32)
        sums = sb("sums", [128, NC * B, C], fp32)
        y_sb = sb("y_sb", [128, 2, TC, D], bf16)
        ffn = sb("ffn", [128, B * T, D], bf16)
        y_out = sb("y_out", [128, NC * B, TC, D], fp32)

        ps = ctx.enter_context(nc.psum_tensor("ps", [128, 8, C], fp32))
        ps_scores = ps[:, 0:4, :].rearrange("p (s b) c -> p s (b c)", s=S_RING)
        ps_max = ps[:, 4:7, :]
        ps_out = ps[:, 7, :]

        x_loaded = [sem(f"x_loaded{b}") for b in range(B)]
        w_loaded = sem("w_loaded")
        f_loaded = sem("f_loaded")
        w_turned = sem("w_turned")
        consts_zero = sem("consts_zero")
        consts = sem("consts")
        rows_set = sem("rows_set")
        norm = sem("norm")
        std_ready = sem("std_ready")
        eps_set = sem("eps_set")
        xn_ready = sem("xn_ready")
        turned = sem("turned")
        xnT_ready = sem("xnT_ready")
        q_ready = sem("q_ready")
        k_ready = sem("k_ready")
        v_ready = sem("v_ready")
        hi_ready = sem("hi_ready")
        v_copied = sem("v_copied")
        qk1_ready = sem("qk1_ready")
        prep_chain = sem("prep_chain")
        part_ready = sem("part_ready")
        parts1_chain = sem("parts1_chain")
        stored = [sem(f"stored{c}") for c in range(NC)]
        row1_stored = sem("row1_stored")
        rows_loaded = [[sem(f"rows_loaded{s}{c}") for c in range(NC)] for s in range(2)]
        v_slot_ready = sem("v_slot_ready")
        scores_ready = sem("scores_ready")
        probs_ready = sem("probs_ready")
        probs_free = sem("probs_free")
        out_ready = sem("out_ready")
        out_free = sem("out_free")
        raw_stored = [sem(f"raw_stored{c}") for c in range(NC)]
        bank_ready = sem("bank_ready")
        bank_free = sem("bank_free")
        max_ready = sem("max_ready")
        max_chain = sem("max_chain")
        max_split = sem("max_split")
        max_rows = [sem(f"max_rows{c}") for c in range(NC)]
        quantised = sem("quantised")
        ffn_chain = sem("ffn_chain")
        ffn_ready = sem("ffn_ready")
        ffn_scaled = sem("ffn_scaled")
        ffn_done = sem("ffn_done")
        att_loaded = [sem(f"att_loaded{n}") for n in range(NC * B)]
        att_ready = sem("att_ready")
        fin_chain = sem("fin_chain")
        y_ready = sem("y_ready")
        y_used = sem("y_used")
        y_out_ready = sem("y_out_ready")
        out_stored = sem("out_stored")

        block = ctx.enter_context(nc.Block())

        x_tiles = x.rearrange("b (t p) d -> b p t d", p=128)
        out_tiles = out.rearrange("b (t p) d -> b p t d", p=128)
        NLOOP = (NG - 2) // 2

        @block.sync
        def _(sp):
            for b in range(B):
                sp.dma_start(xs[:, b * T:(b + 1) * T, :], x_tiles[b]).then_inc(x_loaded[b], 16)
                if b == 0:
                    for n, w in enumerate((wq, wk, wv)):
                        sp.dma_start(w_sb[:, n, :], w).then_inc(w_loaded, 16)

            def load_rows(G, s, c, what):
                for r in range(NP):
                    o = NP * DK * r
                    if "q" in what:
                        sp.dma_start(qr[o:o + NP * DK, s, c, :, :],
                                     parts_dram[0, c, G].rearrange("d p j t -> (d p) j t")).then_inc(rows_loaded[s][c], 16)
                    if "k" in what:
                        sp.dma_start(kr[o:o + NP * DK, s, c, :, :].rearrange("a j t -> a (j t)"),
                                     parts_dram[1, c, G, :, r].rearrange("d j t -> d (j t)").unsqueeze(1)
                                     .broadcast_to([DK, NP, J * C])).then_inc(rows_loaded[s][c], 16)

            for c in range(NC):
                for t in range(2):
                    for p in range(NP):
                        sp.wait_ge(part_ready, NC * NP * c + NP * t + p + 1)
                        sp.dma_start(parts_dram[t, c, 0:GB, :, p, :, :].rearrange("g d j t -> (g d) j t"),
                                     parts[:, t, p, c * C:(c + 1) * C]).then_inc(stored[c], 16)
            for G in range(2):
                for c in range(NC):
                    sp.wait_ge(stored[c], 16 * 2 * NP)
                    if c == 0:
                        sp.wait_ge(rows_set, 2)
                    load_rows(G, G, c, "qk")

            def store_raw(G, c, done):
                sp.wait_ge(out_free, done + 1)
                sp.dma_start(raw_dram[G, :, c * C:(c + 1) * C], raw_sb[:, c, :]).then_inc(raw_stored[c], 16)

            def store_max_rows(G, s, c):
                sp.wait_ge(max_split, NC * G + c + 1)
                for p in range(NP):
                    sp.dma_start(qr[PAD_ROWS + p:PAD_ROWS + p + 1, s, c, :, :].rearrange("a j t -> a (j t)"),
                                 max_parts[:, c, p, :]).then_inc(max_rows[c], 16)

            def group(G, s, loads, maxima):
                if loads:
                    sp.wait_ge(scores_ready, NSTEP * G + Q0_FREE)
                    load_rows(G + 2, s, 0, "q")
                store_raw(G, 0, NC * G + 1)
                if maxima:
                    store_max_rows(G + 1, 1 - s, 0)
                if loads:
                    sp.wait_ge(scores_ready, NSTEP * G + K0_FREE)
                    load_rows(G + 2, s, 0, "k")
                if maxima:
                    store_max_rows(G + 1, 1 - s, 1)
                if loads:
                    sp.wait_ge(scores_ready, NSTEP * (G + 1))
                    load_rows(G + 2, s, 1, "qk")

            def group_end(G):
                store_raw(G, 1, NC * G + 2)

            for c in range(NC):
                store_max_rows(0, 0, c)
            sp.wait_ge(row1_stored, 16 * 2 * NP * NC)
            with sp.Fori(0, NLOOP) as it:
                for s in range(2):
                    group(2 * it + s, s, True, True)
                    group_end(2 * it + s)
            group(NG - 2, 0, False, True)
            group_end(NG - 2)

            def load_att(b, c):
                src = raw_dram[b * GB:(b + 1) * GB, :, c * C:(c + 1) * C].rearrange("g (j r) t -> (g j) r t", j=J)
                n = b * NC + c
                sp.dma_start(att[:, n, :], src[:, 0:DK, :]).then_inc(att_loaded[n], 16)
                sp.dma_start(sums[:, n, :], src[:, DK:2 * DK, :]).then_inc(att_loaded[n], 16)

            for c in range(NC):
                sp.wait_ge(raw_stored[c], 16 * (GB + 1))
                load_att(0, c)
            group(NG - 1, 1, False, False)
            sp.wait_ge(raw_stored[0], 16 * (NG + 1))
            load_att(1, 0)

            def store_out(n):
                sp.wait_ge(y_out_ready, n + 1)
                b, c = divmod(n, NC)
                sp.dma_start(out_tiles[b, :, c * TC:(c + 1) * TC, :], y_out[:, n, :, :]).then_inc(out_stored, 16)

            store_out(0)
            store_out(1)
            group_end(NG - 1)
            sp.wait_ge(raw_stored[1], 16 * (NG + 1))
            load_att(1, 1)
            store_out(2)
            store_out(3)
            sp.wait_ge(out_stored, 16 * NC * B)

        @block.gpsimd
        def _(pool):
            pool.memset(identf[:], 0.0).then_inc(consts_zero, 1)
            pool.memset(identb[:], 0.0).then_inc(consts_zero, 1)
            pool.memset(mask_qk[:], 0.0).then_inc(consts_zero, 1)
            pool.memset(mask_kq[:], 0.0).then_inc(consts_zero, 1)
            pool.wait_ge(consts_zero, 4)
            for m in (identf, identb):
                pool.affine_select(out=m[:], in_=m[:], compare_op=ALU.not_equal, fill=1.0, base=0,
                                   pattern=[[-1, 128]], channel_multiplier=1).then_inc(consts, 1)
            pool.affine_select(out=mask_qk[:], in_=mask_qk[:], compare_op=ALU.is_ge, fill=MASKED, base=0,
                               pattern=[[-1, 128]], channel_multiplier=1).then_inc(consts, 1)
            pool.affine_select(out=mask_kq[:], in_=mask_kq[:], compare_op=ALU.is_ge, fill=MASKED, base=0,
                               pattern=[[1, 128]], channel_multiplier=-1).then_inc(consts, 1)
            pool.wait_ge(consts, 4)
            pool.memset(qr[64:PAD_ROWS].rearrange("p s c j t -> p (s c j t)").bitcast(u32), 0).then_inc(rows_set, 1)
            pool.wait_ge(rows_set, 2)
            pool.memset(vr[:], 1.0).then_inc(rows_set, 1)
            for n, w in enumerate((s_in, s_k)):
                pool.dma_start(scales[:, n:n + 1], w.rearrange("(a n) -> a n", a=1).broadcast_to([128, 1])).then_inc(f_loaded, 16)
            pool.dma_start(bias_sb[:], bias.rearrange("(a n) -> a n", a=1).broadcast_to([128, D])).then_inc(f_loaded, 16)
            pool.dma_start(wf_sb[:], wf).then_inc(f_loaded, 16)
            pool.dma_start(w_sb[:, 3, :], wo).then_inc(f_loaded, 16)

            done = 0
            for t in range(2):
                pool.wait_ge(qk1_ready, 2 * (NC - 1) + t + 1)
                src = qk1[:, t, :]
                to = [parts[:, t, p, S:2 * S] for p in range(NP)]
                for step in range(4):
                    if step == 0:
                        ins = pool.tensor_copy(to[0], src)
                    elif step == 1:
                        ins = pool.tensor_tensor(src, src, to[0], ALU.subtract)
                    elif step == 2:
                        ins = pool.tensor_copy(to[1], src)
                    else:
                        ins = pool.tensor_tensor(to[2], src, to[1], ALU.subtract)
                    done += 1
                    ins.then_inc(parts1_chain, 1)
                    pool.wait_ge(parts1_chain, done)
                for c in range(NC):
                    for p in range(NP):
                        pool.dma_start(parts_dram[t, c, GB:NG, :, p, :, :].rearrange("g d j t -> (g d) j t"),
                                       parts[:, t, p, S + c * C:S + (c + 1) * C]).then_inc(row1_stored, 16)

            pool.wait_ge(f_loaded, 16 * 5)
            pool.wait_ge(norm, 3)
            pool.wait_ge(xnT_ready, B * NC)
            pool.tensor_copy(xnTb[:], xnT[:]).then_inc(ffn_chain, 1)
            pool.wait_ge(ffn_chain, 1)
            done = 1
            work = [(wf_sb[:, :], kq[:, :], 1)] + [
                (xnTb[:, n * C:(n + 1) * C], xq[:, n * C:(n + 1) * C], 0) for n in range(B * NC)]
            count = 0
            for src, dst, n in work:
                w = src.shape[1]
                a, bb, cc, big, small = f_a[:, 0:w], f_b[:, 0:w], f_c[:, 0:w], f8_big[:, 0:w], f8_small[:, 0:w]
                for ins in (
                    lambda: pool.tensor_scalar(a, src, half_inverse[:, n:n + 1], FP8_TOP, ALU.mult, ALU.min),
                    lambda: pool.tensor_scalar(a, a, -FP8_TOP, None, ALU.max),
                    lambda: pool.tensor_copy(big, a, saturate=False),
                    lambda: pool.tensor_copy(cc, big),
                    lambda: pool.tensor_scalar(bb, cc, -0.5, 0.5, ALU.max, ALU.min),
                    lambda: pool.tensor_tensor(cc, cc, bb, ALU.subtract),
                    lambda: pool.tensor_scalar(cc, cc, 2.0, None, ALU.mult),
                    lambda: pool.tensor_scalar(a, src, inverse[:, n:n + 1], 1.0, ALU.mult, ALU.min),
                    lambda: pool.tensor_scalar(a, a, -1.0, None, ALU.max),
                    lambda: pool.tensor_copy(small, a, saturate=False),
                    lambda: pool.tensor_tensor(cc, cc, small, ALU.add),
                    lambda: pool.tensor_scalar(a, cc, OVERFLOW, None, ALU.mult),
                    lambda: pool.tensor_tensor(bb, a, a, ALU.subtract),
                ):
                    ins().then_inc(ffn_chain, 1)
                    done += 1
                    pool.wait_ge(ffn_chain, done)
                pool.tensor_tensor(dst, cc, bb, ALU.add).then_inc(quantised, 1)
                count += 1
                pool.wait_ge(quantised, count)

            for n in range(B * NC):
                pool.wait_ge(ffn_scaled, n + 1)
                pool.tensor_tensor(ffn[:, n * TC:(n + 1) * TC, :], y_sb[:, n % 2, :, :],
                                   bias_sb[:, :].unsqueeze(1).broadcast_to([128, TC, D]), ALU.add).then_inc(ffn_done, 1)

        @block.scalar
        def _(act):
            act.wait_ge(w_loaded, 48)
            for n in range(2):
                act.activation(w_qk[:, n, :].rearrange("p (g d j) -> p g d j", g=GB, j=J),
                               w_sb[:, n, :].rearrange("p (g j d) -> p g d j", g=GB, j=J), ACT.Copy).then_inc(w_turned, 1)
            for b in range(B):
                act.wait_ge(norm, b + 1)
                act.wait_ge(eps_set, 1)
                act.activation(std[:, b * T:(b + 1) * T], moments[:, b * T:(b + 1) * T, 1], ACT.Sqrt,
                               bias=eps[:, 0:1]).then_inc(std_ready, 1)
                for c in range(NC):
                    n = b * NC + c
                    act.wait_ge(turned, n + 1)
                    act.activation(xnT[:, n * C:(n + 1) * C], ps[:, n, :], ACT.Copy).then_inc(xnT_ready, 1)
                for c in range(NC):
                    n = b * NC + c
                    bq, bk, bv = PREP_BANKS[n]
                    if b == 0:
                        act.wait_ge(q_ready, n + 1)
                        act.activation(parts[:, 0, 0, n * C:(n + 1) * C], ps[:, bq, :], ACT.Copy).then_inc(hi_ready, 1)
                        act.wait_ge(k_ready, n + 1)
                        act.activation(parts[:, 1, 0, n * C:(n + 1) * C], ps[:, bk, :], ACT.Copy).then_inc(hi_ready, 1)
                    else:
                        act.wait_ge(q_ready, n + 1)
                        act.activation(qk1[:, 0, c * C:(c + 1) * C], ps[:, bq, :], ACT.Copy).then_inc(qk1_ready, 1)
                        act.wait_ge(k_ready, n + 1)
                        act.activation(qk1[:, 1, c * C:(c + 1) * C], ps[:, bk, :], ACT.Copy).then_inc(qk1_ready, 1)
                    act.wait_ge(v_ready, n + 1)
                    act.activation(
                        v_all[:, b * GB:(b + 1) * GB, c * TC:(c + 1) * TC, :],
                        ps[:, bv, :].rearrange("p (t g e) -> p g t e", t=TC, g=GB), ACT.Copy).then_inc(v_copied, 1)

            def exp_step(G, n, step):
                act.wait_ge(scores_ready, n + 1)
                act.wait_ge(probs_free, n + 1)
                act.activation(probs[:, step % P_RING, :], ps_scores[:, step % S_RING, :], ACT.Exp,
                               scale=SCALE).then_inc(probs_ready, 1)

            def copy_v(G, s):
                act.activation(vr[:, s, :, :, 0:DK],
                               v_all[:, G, :, :].rearrange("p t (j d) -> p t j d", j=J), ACT.Copy).then_inc(v_slot_ready, 1)

            def copy_out(G, c):
                act.wait_ge(out_ready, NC * G + c + 1)
                act.sem_inc(probs_free, 1)
                act.wait_ge(raw_stored[c], 16 * (G + 1))
                act.activation(raw_sb[:, c, :], ps_out, ACT.Copy).then_inc(out_free, 1)

            def group(G, s, last=False):
                for step in range(2, NSTEP):
                    exp_step(G, NSTEP * G + step, step)
                    if step == 4 and not last:
                        act.wait_ge(probs_free, NSTEP * G + P_RING)
                        copy_v(G + 1, 1 - s)
                    if step == O0_DONE:
                        copy_out(G, 0)
                if not last:
                    for step in range(2):
                        exp_step(G, NSTEP * (G + 1) + step, step)
                    copy_out(G, 1)

            act.wait_ge(v_copied, 2)
            act.wait_ge(rows_set, 3)
            copy_v(0, 0)
            act.sem_inc(probs_free, P_RING)
            act.sem_inc(out_free, 1)
            act.sem_inc(raw_stored[0], 16)
            act.sem_inc(raw_stored[1], 16)
            for step in range(2):
                exp_step(0, step, step)
            with act.Fori(0, NLOOP) as it:
                for s in range(2):
                    group(2 * it + s, s)
            group(NG - 2, 0)
            for step in range(2, 7):
                exp_step(NG - 1, NSTEP * (NG - 1) + step, step)
            copy_out(NG - 1, 0)
            for step in range(7, NSTEP):
                exp_step(NG - 1, NSTEP * (NG - 1) + step, step)
                n = step - 7
                if n < B * NC:
                    act.wait_ge(ffn_ready, n + 1)
                    if n >= 2:
                        act.wait_ge(ffn_done, n - 1)
                    act.activation(y_sb[:, n % 2, :, :], ps_max[:, 0, :].rearrange("p (t d) -> p t d", d=D),
                                   ACT.Copy, scale=scale_both[:, 0:1]).then_inc(ffn_scaled, 1)
            copy_out(NG - 1, 1)

        @block.vector
        def _(dve):
            dve.memset(eps[:], EPS).then_inc(eps_set, 1)
            dve.memset(kr[64:128].rearrange("p s c j t -> p (s c j t)").bitcast(fp32), BF16_ONES).then_inc(rows_set, 1)
            chain = 0

            def link(ins):
                nonlocal chain
                chain += 1
                ins.then_inc(prep_chain, 1)
                dve.wait_ge(prep_chain, chain)

            def layer_norm(b):
                dve.wait_ge(x_loaded[b], 16)
                tiles = range(b * T, (b + 1) * T)
                for n in tiles:
                    last = dve.bn_stats(stats[:, n, :], xs[:, n, :])
                link(last)
                for n in tiles:
                    last = dve.bn_aggr(moments[:, n, :], stats[:, n, :])
                last.then_inc(norm, 1)
                dve.wait_ge(std_ready, b + 1)
                link(dve.reciprocal(rstd[:, b * T:(b + 1) * T], std[:, b * T:(b + 1) * T]))
                for n in tiles:
                    dve.tensor_scalar(xn[:, n, :], xs[:, n, :], moments[:, n, 0:1], rstd[:, n:n + 1],
                                      ALU.subtract, ALU.mult).then_inc(xn_ready, 1)

            def split(c):
                for t in range(2):
                    bank = PREP_BANKS[c][t]
                    cols = slice(c * C, (c + 1) * C)
                    done = NC * NP * c + NP * t
                    dve.wait_ge(hi_ready, 2 * c + t + 1)
                    dve.tensor_tensor(rest[:, t, :], ps[:, bank, :], parts[:, t, 0, cols], ALU.subtract).then_inc(part_ready, 1)
                    dve.wait_ge(part_ready, done + 1)
                    dve.tensor_copy(parts[:, t, 1, cols], rest[:, t, :]).then_inc(part_ready, 1)
                    dve.wait_ge(part_ready, done + 2)
                    dve.tensor_tensor(parts[:, t, 2, cols], rest[:, t, :], parts[:, t, 1, cols], ALU.subtract).then_inc(part_ready, 1)
                    dve.wait_ge(part_ready, done + 3)

            layer_norm(0)
            for c in range(NC):
                split(c)
            layer_norm(1)
            dve.wait_ge(f_loaded, 16 * 5)
            link(dve.reciprocal(inverse[:], scales[:]))
            link(dve.tensor_scalar(half_inverse[:], inverse[:], 0.5, None, ALU.mult))
            dve.tensor_tensor(scale_both[:], scales[:, 0:1], scales[:, 1:2], ALU.mult).then_inc(norm, 1)

            CHAIN = 2 * 4 + 1

            def maxima(G):
                links = 0

                def linked(ins):
                    nonlocal links
                    links += 1
                    ins.then_inc(max_chain, 1)
                    dve.wait_ge(max_chain, CHAIN * G + links)

                for n, unit in enumerate(RING):
                    dve.wait_ge(bank_ready, NR * G + n + 1)
                    bank = ps_max[:, n % A_RING, :]
                    if unit[0] == TURN:
                        c = unit[1]
                        rows = bank[0:J * TC, 0:128]
                        if not (isinstance(G, int) and G == 0):
                            dve.wait_ge(max_rows[c], 16 * NP * G)
                        to = [max_parts[:, c, p, :] for p in range(NP)]
                        linked(dve.tensor_copy(to[0], rows))
                        ins = dve.tensor_tensor(max_rest[:], rows, to[0], ALU.subtract)
                        linked(ins)
                        dve.sem_inc(bank_free, 1 + (RING_ADD if n == len(RING) - 1 else 0))
                        linked(dve.tensor_copy(to[1], max_rest[:]))
                        linked(dve.tensor_tensor(to[2], max_rest[:], to[1], ALU.subtract))
                        dve.sem_inc(max_split, 1)
                        continue
                    c, _, reductions = unit
                    for col, segs, length, j, i, part in reductions:
                        src = bank[:, col:col + segs * length].rearrange("p (a b) -> p a b", a=segs)
                        at = J * 0 + j * TC + i % TC
                        end = at + TC * (segs - 1) + 1
                        if part is None:
                            last = dve.tensor_reduce(neg_max[:, 0, at:end:TC], src, AX.X, ALU.max, negate=True)
                        else:
                            last = dve.tensor_reduce(part_max[:, at:end:TC, part], src, AX.X, ALU.max)
                    last.then_inc(bank_free, 1)
                    if n == N0 - 1:
                        dve.wait_ge(bank_free, NR * G + n + 1 + A_RING)
                        dve.sem_inc(max_ready, 1)
                    if n == len(RING) - 2:
                        dve.wait_ge(bank_free, NR * G + n + 1 + A_RING)
                        linked(dve.tensor_reduce(neg_max[:, 1, :], part_max[:], AX.X, ALU.max, negate=True))
                        dve.sem_inc(max_ready, 1)

            dve.sem_inc(bank_free, A_RING)
            maxima(0)
            with dve.Fori(0, NLOOP) as it:
                for s in range(2):
                    maxima(2 * it + s + 1)
            maxima(NG - 1)

            fin = 0

            def fin_link(ins):
                nonlocal fin
                fin += 1
                ins.then_inc(fin_chain, 1)
                dve.wait_ge(fin_chain, fin)

            def finish_att(n):
                dve.wait_ge(att_loaded[n], 32)
                fin_link(dve.reciprocal(sums[:, n, :], sums[:, n, :]))
                dve.tensor_tensor(att[:, n, :], att[:, n, :], sums[:, n, :], ALU.mult).then_inc(att_ready, 1)

            def finish_out(n):
                dve.wait_ge(y_ready, n + 1)
                tiles = slice(n * TC, (n + 1) * TC)
                ins = dve.tensor_tensor(y_out[:, n, :, :], ps_max[:, 1 + n % 2, :].rearrange("p (t d) -> p t d", d=D),
                                        xs[:, tiles, :], ALU.add)
                ins.then_inc(y_used, 1)
                dve.wait_ge(y_used, n + 1)
                dve.wait_ge(ffn_done, n + 1)
                dve.tensor_tensor(y_out[:, n, :, :], y_out[:, n, :, :], ffn[:, tiles, :], ALU.add).then_inc(y_out_ready, 1)

            finish_att(0)
            finish_att(1)
            finish_out(0)
            finish_out(1)
            finish_att(2)
            finish_out(2)
            finish_att(3)
            finish_out(3)

        @block.tensor
        def _(pe):
            pe.wait_ge(consts, 4)
            pe.wait_ge(w_loaded, 48)
            pe.wait_ge(w_turned, 2)
            for b in range(B):
                for c in range(NC):
                    n = b * NC + c
                    for i in range(TC):
                        pe.wait_ge(xn_ready, n * TC + i + 1)
                        last = pe.transpose(ps[:, n, i * 128:(i + 1) * 128], xn[:, n * TC + i, :], identf[:])
                    last.then_inc(turned, 1)
                for c in range(NC):
                    n = b * NC + c
                    bq, bk, bv = PREP_BANKS[n]
                    pe.wait_ge(xnT_ready, n + 1)
                    if n >= 2:
                        if n == 2:
                            pe.wait_ge(part_ready, 2 * NP)
                            pe.wait_ge(v_copied, 1)
                        if n == 3:
                            pe.wait_ge(part_ready, 4 * NP)
                            pe.wait_ge(v_copied, 2)
                    moving = xnT[:, n * C:(n + 1) * C]
                    pe.matmul(ps[:, bq, :], w_qk[:, 0, :], moving, start=True, stop=True).then_inc(q_ready, 1)
                    pe.matmul(ps[:, bk, :], w_qk[:, 1, :], moving, start=True, stop=True).then_inc(k_ready, 1)
                    for i in range(TC):
                        last = pe.matmul(ps[:, bv, i * 128:(i + 1) * 128], xnT[:, (n * TC + i) * 128:(n * TC + i + 1) * 128],
                                         w_sb[:, 2, :], start=True, stop=True)
                    last.then_inc(v_ready, 1)

            def ring_unit(G, s, n):
                unit = RING[n]
                bank = ps_max[:, n % A_RING, :]
                if unit[0] == TURN:
                    c = unit[1]
                    pe.wait_ge(max_ready, NC * G + c + 1)
                    pe.wait_ge(bank_free, NR * G + n + 1)
                    pe.transpose(bank[0:J * TC, 0:128], neg_max[:, c, :], identf[:]).then_inc(
                        bank_ready, 1 + (RING_ADD if n == len(RING) - 1 else 0))
                    return
                c, pieces, _ = unit
                if n == 0 or n == N0:
                    half = G // 2 if isinstance(G, int) else None
                pe.wait_ge(bank_free, NR * G + n + 1)
                for col, j, i, k0, nk, diag in pieces:
                    width = nk * 128
                    q0 = (i % TC) * 128
                    last = pe.matmul(bank[:, col:col + width], qr[0:PAD_ROWS, s, i // TC, j, q0:q0 + 128],
                                     kr[0:PAD_ROWS, s, k0 // TC, j, (k0 % TC) * 128:(k0 % TC) * 128 + width],
                                     start=True, stop=not diag)
                    if diag:
                        last = pe.matmul(bank[:, col + width - 128:col + width], identb[:], mask_qk[:],
                                         start=False, stop=True)
                last.then_inc(bank_ready, 1)

            def pass_a(G, s, turn, ns):
                for n in ns:
                    if n == 0:
                        pe.wait_ge(rows_loaded[s][0], 16 * 2 * NP * (turn + 1))
                    if n == N0:
                        pe.wait_ge(rows_loaded[s][1], 16 * 2 * NP * (turn + 1))
                    ring_unit(G, s, n)

            def scores(G, s, n, step):
                c, pieces = STEPS[step]
                if step == 0 or step == Q0_FREE:
                    pe.wait_ge(max_rows[c], 16 * NP * (G + 1))
                if not (isinstance(n, int) and n < S_RING):
                    pe.wait_ge(probs_ready, n + 1 - S_RING)
                for col, j, kb, q0, width, diag in pieces:
                    to = ps_scores[:, step % S_RING, :]
                    last = pe.matmul(to[:, col:col + width],
                                     kr[0:MAX_ROWS, s, kb // TC, j, (kb % TC) * 128:(kb % TC) * 128 + 128],
                                     qr[0:MAX_ROWS, s, c, j, q0:q0 + width], start=True, stop=not diag)
                    if diag:
                        last = pe.matmul(to[:, col:col + 128], identb[:], mask_kq[:], start=False, stop=True)
                last.then_inc(scores_ready, 1)

            def values(G, s, place, between):
                steps = VALUES.get(place)
                if steps is None:
                    between()
                    return
                c = STEPS[steps[0]][0]
                first, final = steps[0] in (0, Q0_FREE), steps[-1] in (Q0_FREE - 1, NSTEP - 1)
                if steps[0] == 0:
                    pe.wait_ge(v_slot_ready, G + 1)
                if first:
                    pe.wait_ge(out_free, NC * G + c + 1)
                pe.wait_ge(probs_ready, NSTEP * G + steps[-1] + 1)
                todo = sorted(((k, step, p) for step in steps for k, p in enumerate(
                    sorted(STEPS[step][1], key=lambda p: (p[2], p[1])))), key=lambda e: (e[2][2], e[2][1]))
                for m, (_, step, (col, j, kb, q0, width, _)) in enumerate(todo):
                    if m == len(todo) // 2:
                        between()
                    ins = pe.matmul(ps_out[32 * j:32 * j + 32, q0:q0 + width], vr[:, s, kb, j, :],
                                    probs[:, step % P_RING, col:col + width], start=(kb == 0), stop=(kb == TC * c + 2),
                                    skip_group_check=True)
                if final:
                    ins.then_inc(out_ready, 1)
                else:
                    ins.then_inc(probs_free, len(steps))

            def group(G, s, turn, following=True, extra=None):
                for place in range(2, NSTEP + 2):
                    if place < NSTEP:
                        scores(G, s, NSTEP * G + place, place)
                    elif following:
                        scores(G + 1, 1 - s, NSTEP * (G + 1) + place - NSTEP, place - NSTEP)
                    ns = PLACES.get(place, []) if following else []
                    last = ns[-1:] if place < LAST_PLACE else []
                    if place < LAST_PLACE:
                        pass_a(G + 1, 1 - s, turn, ns[:-1])
                    values(G, s, place, lambda: pass_a(G + 1, 1 - s, turn, last))
                    if place == LAST_PLACE:
                        pass_a(G + 1, 1 - s, turn, ns)
                    if extra:
                        extra(place)

            pe.wait_ge(v_copied, B * NC)
            pass_a(0, 0, 0, range(len(RING)))
            for step in range(2):
                scores(0, 0, step, step)
            with pe.Fori(0, NLOOP) as it:
                for s in range(2):
                    group(2 * it + s, s, it + s)
            group(NG - 2, 0, NG // 2 - 1)

            def dense(n):
                if n == 0:
                    pe.wait_ge(bank_free, NR * NG + A_RING)
                    pe.wait_ge(quantised, 1 + B * NC)
                else:
                    pe.wait_ge(ffn_scaled, n)
                for i in range(TC):
                    t = n * TC + i
                    last = pe.matmul(ps_max[:, 0, i * 128:(i + 1) * 128], xq[:, t * 128:(t + 1) * 128], kq[:],
                                     start=True, stop=True)
                last.then_inc(ffn_ready, 1)

            def project(n):
                pe.wait_ge(att_ready, n + 1)
                if n >= 2:
                    pe.wait_ge(y_used, n - 1)
                if n == 0:
                    pe.wait_ge(f_loaded, 16 * 5)
                for i in range(TC):
                    last = pe.matmul(ps_max[:, 1 + n % 2, i * 128:(i + 1) * 128], att[:, n, i * 128:(i + 1) * 128],
                                     w_sb[:, 3, :], start=True, stop=True)
                last.then_inc(y_ready, 1)

            def last_group_extra(place):
                if 7 <= place < 7 + B * NC:
                    dense(place - 7)
                if place == 11:
                    project(0)
                if place == 13:
                    project(1)

            group(NG - 1, 1, 0, following=False, extra=last_group_extra)
            project(2)
            project(3)


PREP_BANKS = [(4, 5, 6), (7, 0, 1), (4, 5, 6), (7, 0, 1)]

_INS = ['L0_attn_x', 'L0_attn_WQ', 'L0_attn_WK', 'L0_attn_WV', 'L0_attn_WO', 'L0_ffn_kernel',
        'L0_ffn_input_scale', 'L0_ffn_kernel_scale', 'L0_ffn_bias']


def kernel(**inputs):
    import numpy as _np
    import concourse.bacc as _bacc
    from concourse import mybir as _mybir
    from concourse.bass_utils import run_bass_kernel_spmd as _run

    nc = _bacc.Bacc("TRN2", target_bir_lowering=False, num_devices=1)
    arrays, args = {}, []
    for name in _INS:
        a = _np.ascontiguousarray(inputs[name])
        arrays[f"in_{name}"] = a
        args.append(nc.dram_tensor(f"in_{name}", a.shape, _mybir.dt.from_np(a.dtype), kind="ExternalInput").ap())
    out = nc.dram_tensor("out", (B, S, D), fp32, kind="ExternalOutput").ap()
    attention_kernel(nc, *args, out)
    r = _run(nc, [arrays], core_ids=[0])
    return r.results[0]["out"]
```

```python
import concourse.bass as bass
from concourse import mybir
from contextlib import ExitStack

fp32 = mybir.dt.float32
bf16 = mybir.dt.bfloat16
fp8 = mybir.dt.float8e4
u32 = mybir.dt.uint32
ALU = mybir.AluOpType
ACT = mybir.ActivationFunctionType
AX = mybir.AxisListType

B, S, D = 2, 1024, 128
H = 16
DK = D // H
J = 4
GB = H // J
NG = B * GB
T = S // 128
C = 512
NC = S // C
TC = C // 128
NP = 3
SPLIT_ROWS = NP * NP * DK
PAD_ROWS = 96
MAX_ROWS = PAD_ROWS + NP
VW = 32
MASKED = -3.0e38
EPS = 1e-5
SCALE = float(DK) ** -0.5
BF16_ONES = 1.0019378662109375
FP8_TOP = 240.0
OVERFLOW = 7.3e35
P_RING = 6
FX = B * S // NG
FIRST = 4
A_FIRST = 0
S_RING = 2
A_RING = 3
UNUSED = A_RING + 1


def score_steps():
    steps = []
    for c in range(NC):
        first = TC * c
        for kb in range(first + 1):
            for pair in range(2):
                steps.append((c, [(C * n, 2 * pair + n, kb, 0, C, kb == first) for n in range(2)]))
        for pair in range(2):
            steps.append((c, [p for n in range(2) for p in (
                (C * n, 2 * pair + n, first + 1, 128, 384, True),
                (C * n + 384, 2 * pair + n, first + 3, 384, 128, True))]))
        steps.append((c, [(256 * j, j, first + 2, 256, 256, True) for j in range(J)]))
    return steps


def max_units():
    units = []
    for pair in (0, 2):
        for j in (pair, pair + 1):
            units.append((0, [(0, j, 3, 0, 4, True, None)]))
        for j in (pair, pair + 1):
            units.append((0, [(0, j, 2, 0, 3, True, None), (384, j, 0, 0, 1, True, None)]))
        units.append((0, [(256 * n, pair + n, 1, 0, 2, True, None) for n in range(2)]))
    for pair in (0, 2):
        for j in (pair, pair + 1):
            for i in range(4, 8):
                units.append((1, [(0, j, i, 0, 4, False, 0)]))
            units.append((1, [(0, j, 7, 4, 4, True, 1)]))
            units.append((1, [(0, j, 6, 4, 3, True, 1), (384, j, 4, 4, 1, True, 1)]))
        units.append((1, [(256 * n, pair + n, 5, 4, 2, True, 1) for n in range(2)]))
    return units


STEPS = score_steps()
MASKED_STEPS = [n for n, (_, pieces) in enumerate(STEPS) if pieces[0][5]]
NSTEP = len(STEPS)
UNITS = max_units()
N0 = sum(c == 0 for c, _ in UNITS)
TURN = "turn"
RING = UNITS[:4] + [(TURN, 1)] + UNITS[4:N0 + NP + 3] + [(TURN, 0)] + UNITS[N0 + NP + 3:]
TURN_AT = [RING.index((TURN, c)) for c in range(NC)]
C0_LAST, C1_FIRST = RING.index(UNITS[N0 - 1]), RING.index(UNITS[N0])
RING_ADD = -len(RING) % A_RING
NR = len(RING) + RING_ADD
Q0_FREE = sum(c == 0 for c, _ in STEPS)
K0_FREE = Q0_FREE + 2 * TC
VALUES = {}
_s = 0
while _s < NSTEP:
    _n = 1 if _s + 1 == NSTEP or STEPS[_s + 1][0] != STEPS[_s][0] else 2
    VALUES[_s + _n - 1 + 2] = list(range(_s, _s + _n))
    _s += _n
O0_DONE = Q0_FREE - 1 + 2


def values_place(place):
    return place if place < NSTEP + 2 else place - NSTEP


def value_pieces(place):
    return sorted(((step, p) for step in VALUES.get(place, []) for p in STEPS[step][1]),
                  key=lambda e: (e[1][2], e[0], e[1][1]))


def spread_units():
    spots, at = [], 0
    for place in range(A_FIRST, NSTEP + A_FIRST):
        at += sum(piece[4] for piece in STEPS[place % NSTEP][1])
        spots.append((at, (place, 0)))
        for m, (_, piece) in enumerate(value_pieces(values_place(place))):
            at += piece[4] * PV_COST
            spots.append((at, (place, m + 1)))
    need = [TURN_COST if unit[0] == TURN else sum(128 * p[4] + 64 for p in unit[1]) for unit in RING]
    where, spent = {}, 0
    for n in range(len(RING)):
        due = at * SPAN * spent / sum(need)
        where.setdefault(min(spot for spot in spots if spot[0] >= due)[1], []).append(n)
        spent += need[n]
    return where


PV_COST = 1.25
TURN_COST = 800
SPAN = 1.0
SPREAD = spread_units()


def attention_kernel(nc, x, wq, wk, wv, wo, wf, s_in, s_k, bias, out):
    ctx = ExitStack()
    with ctx:
        def sb(name, shape, dt):
            return ctx.enter_context(nc.sbuf_tensor(name, shape, dt))

        def sem(name):
            return ctx.enter_context(nc.semaphore(name))

        parts_dram = nc.dram_tensor("parts_dram", (2, NC, NG, DK, NP, J, C), bf16, kind="Internal").ap()
        raw_dram = nc.dram_tensor("raw_dram", (NG, 128, S), fp32, kind="Internal").ap()

        xs = sb("xs", [128, B * T, D], fp32)
        xn = sb("xn", [128, B * T, D], fp32)
        stats = sb("stats", [128, B * T, 6], fp32)
        moments = sb("moments", [128, B * T, 2], fp32)
        std = sb("std", [128, B * T], fp32)
        rstd = sb("rstd", [128, B * T], fp32)
        eps = sb("eps", [128, 1], fp32)
        w_sb = sb("w_sb", [128, 4, D], fp32)
        w_qk = sb("w_qk", [128, 2, D], fp32)
        wf_sb = sb("wf_sb", [128, D], bf16)
        bias_sb = sb("bias_sb", [128, D], bf16)
        scales = sb("scales", [128, 2], fp32)
        inverse = sb("inverse", [128, 2], fp32)
        half_inverse = sb("half_inverse", [128, 2], fp32)
        scale_both = sb("scale_both", [128, 1], fp32)
        identf = sb("identf", [128, 128], fp32)
        ident = sb("ident", [128, 128], bf16)
        mask_qk = sb("mask_qk", [128, C], bf16)
        xnT = sb("xnT", [128, B * S], fp32)
        parts = sb("parts", [128, 2, NP, B * S], bf16)
        rest = sb("rest", [128, 2, C], fp32)
        qk1 = sb("qk1", [128, 2, S], fp32)
        v_all = sb("v_all", [128, NG, T, 32], fp32)
        xq = sb("xq", [128, B * S], bf16)
        kq = sb("kq", [128, D], bf16)
        f_x = sb("f_x", [128, FX], bf16)
        f_a = sb("f_a", [128, FX], fp32)
        f_b = sb("f_b", [128, FX], fp32)
        f_c = sb("f_c", [128, FX], fp32)
        f8_big = sb("f8_big", [128, FX], fp8)
        f8_small = sb("f8_small", [128, FX], fp8)

        qr = sb("qr", [128, 2, NC, J, C], bf16)
        kr = sb("kr", [128, 2, NC, J, C], bf16)
        vr = sb("vr", [128, 2, T, J, VW], fp32)
        probs = sb("probs", [128, P_RING, 2 * C], fp32)
        part_min = sb("part_min", [128, J * TC, 2], fp32)
        unused = sb("unused", [128, UNUSED, 2, C], bf16)
        neg_max = sb("neg_max", [128, NC, J * TC], fp32)
        max_rest = sb("max_rest", [128, NC, J * TC], fp32)
        max_parts = sb("max_parts", [128, NC, 128], bf16)
        max_turned = sb("max_turned", [NP * J * TC, NC, 128], bf16)
        raw_sb = sb("raw_sb", [128, NC, C], fp32)
        att = sb("att", [128, NC * B, C], fp32)
        sums = sb("sums", [128, NC * B, C], fp32)
        y_sb = sb("y_sb", [128, NC * B, TC, D], bf16)
        ffn = sb("ffn", [128, B * T, D], bf16)
        y_out = sb("y_out", [128, NC * B, TC, D], fp32)

        ps = ctx.enter_context(nc.psum_tensor("ps", [128, 8, C], fp32))
        ps_scores = ps[:, 0:4, :].rearrange("p (s b) c -> p s (b c)", s=S_RING)
        ps_max = ps[:, 4:7, :]
        ps_out = ps[:, 7, :]

        x_loaded = [sem(f"x_loaded{n}") for n in range(B * NC)]
        w_loaded = sem("w_loaded")
        f_loaded = sem("f_loaded")
        w_turned = sem("w_turned")
        consts_zero = sem("consts_zero")
        consts = sem("consts")
        rows_set = sem("rows_set")
        norm = sem("norm")
        std_ready = sem("std_ready")
        eps_set = sem("eps_set")
        xn_ready = sem("xn_ready")
        turned = sem("turned")
        xnT_ready = sem("xnT_ready")
        q_ready = sem("q_ready")
        k_ready = sem("k_ready")
        v_ready = sem("v_ready")
        hi_ready = sem("hi_ready")
        v_copied = sem("v_copied")
        qk1_ready = sem("qk1_ready")
        prep_chain = sem("prep_chain")
        part_ready = sem("part_ready")
        rest1_ready = sem("rest1_ready")
        middle_ready = sem("middle_ready")
        low_ready = sem("low_ready")
        stored = [sem(f"stored{c}") for c in range(NC)]
        row1_stored = sem("row1_stored")
        rows_loaded = [[sem(f"rows_loaded{s}{c}") for c in range(NC)] for s in range(2)]
        v_slot_ready = sem("v_slot_ready")
        scores_ready = sem("scores_ready")
        probs_ready = sem("probs_ready")
        probs_masked = sem("probs_masked")
        mask_begun = sem("mask_begun")
        max_begun = sem("max_begun")
        probs_free = sem("probs_free")
        out_ready = sem("out_ready")
        out_free = sem("out_free")
        raw_stored = [sem(f"raw_stored{c}") for c in range(NC)]
        bank_ready = sem("bank_ready")
        bank_free = sem("bank_free")
        max_ready = sem("max_ready")
        max_chain = sem("max_chain")
        max_rows = [sem(f"max_rows{c}") for c in range(NC)]
        factors_ready = sem("factors_ready")
        quantised = sem("quantised")
        ffn_ready = sem("ffn_ready")
        ffn_scaled = sem("ffn_scaled")
        ffn_done = sem("ffn_done")
        att_loaded = [sem(f"att_loaded{n}") for n in range(NC * B)]
        att_ready = sem("att_ready")
        fin_chain = sem("fin_chain")
        y_ready = sem("y_ready")
        y_used = sem("y_used")
        y_out_ready = sem("y_out_ready")
        out_stored = sem("out_stored")

        block = ctx.enter_context(nc.Block())

        x_tiles = x.rearrange("b (t p) d -> b p t d", p=128)
        out_tiles = out.rearrange("b (t p) d -> b p t d", p=128)
        NLOOP = (NG - 2) // 2

        def turned_view(bank):
            return bank[:, 0:64].bitcast(bf16)

        def store_part(eng, t, b, c, p, done):
            eng.dma_start(parts_dram[t, c, b * GB:(b + 1) * GB, :, p, :, :].rearrange("g d j t -> (g d) j t"),
                          parts[:, t, p, b * S + c * C:b * S + (c + 1) * C]).then_inc(done, 16)

        @block.sync
        def _(sp):
            for n in range(B * NC):
                sp.dma_start(xs[:, n * TC:(n + 1) * TC, :], x_tiles[n // NC][:, (n % NC) * TC:(n % NC + 1) * TC, :]
                             ).then_inc(x_loaded[n], 16)
                if n == 0:
                    for m, w in enumerate((wq, wk, wv)):
                        sp.dma_start(w_sb[:, m, :], w).then_inc(w_loaded, 16)
            for n, w in enumerate((s_in, s_k)):
                sp.dma_start(scales[:, n:n + 1], w.rearrange("(a n) -> a n", a=1).broadcast_to([128, 1])).then_inc(f_loaded, 16)
            sp.dma_start(bias_sb[:], bias.rearrange("(a n) -> a n", a=1).broadcast_to([128, D])).then_inc(f_loaded, 16)
            sp.dma_start(wf_sb[:], wf).then_inc(f_loaded, 16)
            sp.dma_start(w_sb[:, 3, :], wo).then_inc(f_loaded, 16)

            def load_rows(G, s, c, what):
                for r in range(NP):
                    o = NP * DK * r
                    if "q" in what:
                        sp.dma_start(qr[o:o + NP * DK, s, c, :, :],
                                     parts_dram[0, c, G].rearrange("d p j t -> (d p) j t")).then_inc(rows_loaded[s][c], 16)
                    if "k" in what:
                        sp.dma_start(kr[o:o + NP * DK, s, c, :, :].rearrange("a j t -> a (j t)"),
                                     parts_dram[1, c, G, :, r].rearrange("d j t -> d (j t)").unsqueeze(1)
                                     .broadcast_to([DK, NP, J * C])).then_inc(rows_loaded[s][c], 16)

            def store_raw(G, c, done):
                sp.wait_ge(out_free, done + 1)
                sp.dma_start(raw_dram[G, :, c * C:(c + 1) * C], raw_sb[:, c, :]).then_inc(raw_stored[c], 16)

            def store_max_rows(G, s, c):
                sp.wait_ge(bank_free, A_RING + NR * (G + c) + TURN_AT[c] + 1)
                sp.dma_start(qr[PAD_ROWS:PAD_ROWS + NP, s, c, :, :].rearrange("p j t -> p (j t)"),
                             max_turned[:, c, :]).then_inc(max_rows[c], 16)

            def group(G, s, loads, maxima):
                if loads:
                    sp.wait_ge(scores_ready, NSTEP * G + Q0_FREE)
                    load_rows(G + 2, s, 0, "q")
                store_raw(G, 0, NC * G + 1)
                if maxima:
                    store_max_rows(G + 1, 1 - s, 0)
                if loads:
                    sp.wait_ge(scores_ready, NSTEP * G + K0_FREE)
                    load_rows(G + 2, s, 0, "k")
                if loads:
                    sp.wait_ge(scores_ready, NSTEP * (G + 1))
                    load_rows(G + 2, s, 1, "qk")
                store_raw(G, 1, NC * G + 2)
                if maxima:
                    store_max_rows(G + 1, 1 - s, 1)

            for t in range(2):
                for p in range(NP):
                    sp.wait_ge(part_ready, NP * t + p + 1)
                    store_part(sp, t, 0, 0, p, stored[0])
            sp.wait_ge(rows_set, 2)
            for c in range(NC):
                sp.wait_ge(stored[c], 16 * 2 * NP)
                load_rows(0, 0, c, "qk")
            store_max_rows(0, 0, 0)
            for c in range(NC):
                load_rows(1, 1, c, "qk")
            for t in range(2):
                for p in range(NP):
                    if p < 2:
                        sp.wait_ge((qk1_ready, middle_ready)[p], (2 * (NC - 1) + t + 1, t + 1)[p])
                    else:
                        sp.wait_ge(low_ready, t + 1)
                    for c in range(NC):
                        store_part(sp, t, 1, c, p, row1_stored)
            store_max_rows(0, 0, 1)
            sp.wait_ge(row1_stored, 16 * 2 * NP * NC)
            with sp.Fori(0, NLOOP) as it:
                for s in range(2):
                    group(2 * it + s, s, True, True)
            group(NG - 2, 0, False, True)

            def load_att(b, c):
                src = raw_dram[b * GB:(b + 1) * GB, :, c * C:(c + 1) * C].rearrange("g (j r) t -> (g j) r t", j=J)
                n = b * NC + c
                sp.dma_start(att[:, n, :], src[:, 0:DK, :]).then_inc(att_loaded[n], 16)
                sp.dma_start(sums[:, n, :], src[:, DK:2 * DK, :]).then_inc(att_loaded[n], 16)

            for c in range(NC):
                sp.wait_ge(raw_stored[c], 16 * (GB + 1))
                load_att(0, c)
            store_raw(NG - 1, 0, NC * (NG - 1) + 1)
            sp.wait_ge(raw_stored[0], 16 * (NG + 1))
            load_att(1, 0)

            def store_out(n):
                sp.wait_ge(y_out_ready, n + 1)
                b, c = divmod(n, NC)
                sp.dma_start(out_tiles[b, :, c * TC:(c + 1) * TC, :], y_out[:, n, :, :]).then_inc(out_stored, 16)

            store_out(0)
            store_out(1)
            store_raw(NG - 1, 1, NC * NG)
            sp.wait_ge(raw_stored[1], 16 * (NG + 1))
            load_att(1, 1)
            store_out(2)
            store_out(3)
            sp.wait_ge(out_stored, 16 * NC * B)

        @block.gpsimd
        def _(pool):
            pool.memset(identf[:], 0.0).then_inc(consts_zero, 1)
            pool.memset(mask_qk[:], 0.0).then_inc(consts_zero, 1)
            pool.wait_ge(consts_zero, 2)
            pool.affine_select(out=identf[:], in_=identf[:], compare_op=ALU.not_equal, fill=1.0, base=0,
                               pattern=[[-1, 128]], channel_multiplier=1).then_inc(consts, 1)
            pool.affine_select(out=mask_qk[:, C - 128:], in_=mask_qk[:, C - 128:], compare_op=ALU.is_ge, fill=MASKED,
                               base=0, pattern=[[-1, 128]], channel_multiplier=1).then_inc(consts, 1)
            pool.wait_ge(consts, 1)
            pool.tensor_copy(ident[:], identf[:]).then_inc(consts, 1)
            pool.wait_ge(consts, 3)
            pool.memset(kr[64:128].rearrange("p s c j t -> p (s c j t)").bitcast(fp32), BF16_ONES).then_inc(rows_set, 1)
            pool.wait_ge(rows_set, 1)
            pool.memset(qr[64:PAD_ROWS].rearrange("p s c j t -> p (s c j t)").bitcast(u32), 0).then_inc(rows_set, 1)
            pool.wait_ge(rows_set, 2)
            pool.memset(vr[:], 1.0).then_inc(rows_set, 1)
            def quantise(src, dst, n):
                w = src.shape[1]
                pool.tensor_scalar(f_a[:, 0:w], src, half_inverse[:, n:n + 1], FP8_TOP, ALU.mult, ALU.min)
                pool.drain()
                pool.tensor_scalar(f_a[:, 0:w], f_a[:, 0:w], -FP8_TOP, None, ALU.max)
                pool.drain()
                pool.tensor_copy(f8_big[:, 0:w], f_a[:, 0:w], saturate=False)
                pool.drain()
                pool.tensor_copy(f_c[:, 0:w], f8_big[:, 0:w])
                pool.drain()
                pool.tensor_scalar(f_b[:, 0:w], f_c[:, 0:w], -0.5, 0.5, ALU.max, ALU.min)
                pool.drain()
                pool.tensor_tensor(f_c[:, 0:w], f_c[:, 0:w], f_b[:, 0:w], ALU.subtract)
                pool.drain()
                pool.tensor_scalar(f_c[:, 0:w], f_c[:, 0:w], 2.0, None, ALU.mult)
                pool.drain()
                pool.tensor_scalar(f_a[:, 0:w], src, inverse[:, n:n + 1], 1.0, ALU.mult, ALU.min)
                pool.drain()
                pool.tensor_scalar(f_a[:, 0:w], f_a[:, 0:w], -1.0, None, ALU.max)
                pool.drain()
                pool.tensor_copy(f8_small[:, 0:w], f_a[:, 0:w], saturate=False)
                pool.drain()
                pool.tensor_tensor(f_c[:, 0:w], f_c[:, 0:w], f8_small[:, 0:w], ALU.add)
                pool.drain()
                pool.tensor_scalar(f_a[:, 0:w], f_c[:, 0:w], OVERFLOW, 0.0, ALU.mult, ALU.mult)
                pool.drain()
                return pool.tensor_tensor(dst, f_c[:, 0:w], f_a[:, 0:w], ALU.add)

            for t in range(2):
                for p in range(NP):
                    pool.wait_ge(part_ready, NC * NP + NP * t + p + 1)
                    store_part(pool, t, 0, 1, p, stored[1])

            pool.wait_ge(f_loaded, 16 * 5)
            pool.wait_ge(factors_ready, 3)
            quantise(wf_sb[:], kq[:], 1)

            for t in range(2):
                pool.wait_ge(qk1_ready, 2 * (NC - 1) + t + 1)
                pool.tensor_tensor(qk1[:, t, :], qk1[:, t, :], parts[:, t, 0, S:2 * S], ALU.subtract).then_inc(rest1_ready, 1)
            for t in range(2):
                pool.wait_ge(middle_ready, t + 1)
                pool.tensor_tensor(parts[:, t, 2, S:2 * S], qk1[:, t, :], parts[:, t, 1, S:2 * S], ALU.subtract
                                   ).then_inc(low_ready, 1)

            def mask_probs(G, step):
                c, pieces = STEPS[step]
                blocks = probs[:, step % P_RING, :]
                if len(pieces) == 2:
                    views = [blocks.rearrange("p (a b) -> p a b", a=2)[:, :, 0:128]]
                elif pieces[1][0] == 384:
                    views = [half.rearrange("p (a b) -> p a b", b=128)[:, 0:4:3, :] for half in (blocks[:, 0:C], blocks[:, C:2 * C])]
                else:
                    views = [blocks.rearrange("p (a b) -> p a b", a=4)[:, :, 0:128]]
                pool.wait_ge(probs_ready, NSTEP * G + step + 1)
                pool.sem_inc(mask_begun, 1)
                for view in views:
                    last = pool.affine_select(out=view, in_=view, compare_op=ALU.is_ge, fill=0.0, base=0,
                                              pattern=[[0, view.shape[1]], [1, 128]], channel_multiplier=-1)
                last.then_inc(probs_masked, 1)

            def quantise_share(n):
                pool.tensor_copy(f_x[:], xnT[:, bass.ts(n, FX)])
                pool.drain()
                return quantise(f_x[:], xq[:, bass.ts(n, FX)], 0)

            def add_bias(n):
                pool.wait_ge(ffn_scaled, n + 1)
                pool.tensor_tensor(ffn[:, n * TC:(n + 1) * TC, :], y_sb[:, n, :, :],
                                   bias_sb[:, :].unsqueeze(1).broadcast_to([128, TC, D]), ALU.add).then_inc(ffn_done, 1)

            def group(G, final_share=False, last=False):
                for step in MASKED_STEPS:
                    if step >= FIRST:
                        mask_probs(G, step)
                    if step == Q0_FREE - 1:
                        if not last:
                            done = quantise_share(G + 1)
                            if final_share:
                                done.then_inc(quantised, 1)
                        else:
                            for n in range(B * NC):
                                add_bias(n)
                if not last:
                    for step in range(FIRST):
                        mask_probs(G + 1, step)

            pool.wait_ge(xnT_ready, B * NC)
            quantise_share(0)
            for step in range(FIRST):
                mask_probs(0, step)
            with pool.Fori(0, NLOOP) as it:
                for s in range(2):
                    group(2 * it + s)
            group(NG - 2, final_share=True)
            group(NG - 1, last=True)

        @block.scalar
        def _(act):
            def take_std(n):
                act.wait_ge(norm, n + 1)
                act.activation(std[:, n * TC:(n + 1) * TC], moments[:, n * TC:(n + 1) * TC, 1], ACT.Sqrt,
                               bias=eps[:, 0:1]).then_inc(std_ready, 1)

            def take_xnT(n):
                act.wait_ge(turned, n + 1)
                act.activation(xnT[:, n * C:(n + 1) * C], ps[:, TURN_BANKS[n], :], ACT.Copy).then_inc(xnT_ready, 1)

            def take_qk(n):
                for t, ready in enumerate((q_ready, k_ready)):
                    bank = ps[:, PREP_BANKS[n][t], :]
                    act.wait_ge(ready, n + 1)
                    hi = act.activation(parts[:, t, 0, n * C:(n + 1) * C], bank, ACT.Copy)
                    if n < NC:
                        hi.then_inc(hi_ready, 1)
                    else:
                        act.activation(qk1[:, t, (n - NC) * C:(n - NC + 1) * C], bank, ACT.Copy).then_inc(qk1_ready, 1)

            def take_v(n):
                b, c = divmod(n, NC)
                act.wait_ge(v_ready, n + 1)
                act.activation(v_all[:, b * GB:(b + 1) * GB, c * TC:(c + 1) * TC, :],
                               ps[:, PREP_BANKS[n][2], :].rearrange("p (t g e) -> p g t e", t=TC, g=GB), ACT.Copy
                               ).then_inc(v_copied, 1)

            act.wait_ge(eps_set, 1)
            take_std(0)
            act.wait_ge(w_loaded, 48)
            for n in range(2):
                act.activation(w_qk[:, n, :].rearrange("p (g d j) -> p g d j", g=GB, j=J),
                               w_sb[:, n, :].rearrange("p (g j d) -> p g d j", g=GB, j=J), ACT.Copy).then_inc(w_turned, 1)
            take_xnT(0)
            take_std(1)
            take_qk(0)
            take_v(0)
            take_xnT(1)
            take_qk(1)
            take_v(1)
            take_std(2)
            take_xnT(2)
            take_std(3)
            take_xnT(3)
            for n in (2, 3):
                take_qk(n)
                take_v(n)
            for t in range(2):
                act.wait_ge(rest1_ready, t + 1)
                act.activation(parts[:, t, 1, S:2 * S], qk1[:, t, :], ACT.Copy).then_inc(middle_ready, 1)

            def exp_step(G, n, step):
                act.wait_ge(scores_ready, n + 1)
                act.wait_ge(probs_free, n + 1)
                act.activation(probs[:, step % P_RING, :], ps_scores[:, step % S_RING, :], ACT.Exp,
                               scale=SCALE).then_inc(probs_ready, 1)

            def copy_v(G, s):
                act.activation(vr[:, s, :, :, 0:DK],
                               v_all[:, G, :, :].rearrange("p t (j d) -> p t j d", j=J), ACT.Copy).then_inc(v_slot_ready, 1)

            def copy_out(G, c):
                act.wait_ge(out_ready, NC * G + c + 1)
                act.sem_inc(probs_free, 1)
                act.wait_ge(raw_stored[c], 16 * (G + 1))
                act.activation(raw_sb[:, c, :], ps_out, ACT.Copy).then_inc(out_free, 1)

            def group(G, s, last=False):
                for step in range(FIRST, NSTEP):
                    exp_step(G, NSTEP * G + step, step)
                    if step == 4 and not last:
                        act.wait_ge(probs_free, NSTEP * G + P_RING)
                        copy_v(G + 1, 1 - s)
                    if step == O0_DONE:
                        copy_out(G, 0)
                if not last:
                    for step in range(FIRST):
                        exp_step(G, NSTEP * (G + 1) + step, step)
                        if step == 1:
                            copy_out(G, 1)

            act.wait_ge(v_copied, 2)
            act.wait_ge(rows_set, 3)
            copy_v(0, 0)
            act.sem_inc(probs_free, P_RING)
            act.sem_inc(out_free, 1)
            act.sem_inc(raw_stored[0], 16)
            act.sem_inc(raw_stored[1], 16)
            for step in range(FIRST):
                exp_step(0, step, step)
            with act.Fori(0, NLOOP) as it:
                for s in range(2):
                    group(2 * it + s, s)
            group(NG - 2, 0)
            for step in range(FIRST, 7):
                exp_step(NG - 1, NSTEP * (NG - 1) + step, step)
            copy_out(NG - 1, 0)
            for step in range(7, NSTEP):
                exp_step(NG - 1, NSTEP * (NG - 1) + step, step)
                n = step - 7
                if n < B * NC:
                    act.wait_ge(ffn_ready, n + 1)
                    act.activation(y_sb[:, n, :, :], ps_max[:, 0, :].rearrange("p (t d) -> p t d", d=D),
                                   ACT.Copy, scale=scale_both[:, 0:1]).then_inc(ffn_scaled, 1)
            copy_out(NG - 1, 1)

        @block.vector
        def _(dve):
            dve.memset(eps[:], EPS).then_inc(eps_set, 1)
            dve.memset(max_parts[:], 0.0).then_inc(eps_set, 1)
            chain = 0

            def link(ins):
                nonlocal chain
                chain += 1
                ins.then_inc(prep_chain, 1)
                dve.wait_ge(prep_chain, chain)

            def layer_norm(n):
                dve.wait_ge(x_loaded[n], 16)
                tiles = range(n * TC, (n + 1) * TC)
                for t in tiles:
                    last = dve.bn_stats(stats[:, t, :], xs[:, t, :])
                link(last)
                for t in tiles:
                    last = dve.bn_aggr(moments[:, t, :], stats[:, t, :])
                last.then_inc(norm, 1)
                dve.wait_ge(std_ready, n + 1)
                link(dve.reciprocal(rstd[:, n * TC:(n + 1) * TC], std[:, n * TC:(n + 1) * TC]))
                for t in tiles:
                    dve.tensor_scalar(xn[:, t, :], xs[:, t, :], moments[:, t, 0:1], rstd[:, t:t + 1],
                                      ALU.subtract, ALU.mult).then_inc(xn_ready, 1)

            def split(c):
                for t in range(2):
                    bank = PREP_BANKS[c][t]
                    cols = slice(c * C, (c + 1) * C)
                    done = NC * NP * c + NP * t
                    dve.wait_ge(hi_ready, 2 * c + t + 1)
                    dve.tensor_tensor(rest[:, t, :], ps[:, bank, :], parts[:, t, 0, cols], ALU.subtract).then_inc(part_ready, 1)
                    dve.wait_ge(part_ready, done + 1)
                    dve.tensor_copy(parts[:, t, 1, cols], rest[:, t, :]).then_inc(part_ready, 1)
                    dve.wait_ge(part_ready, done + 2)
                    dve.tensor_tensor(parts[:, t, 2, cols], rest[:, t, :], parts[:, t, 1, cols], ALU.subtract).then_inc(part_ready, 1)
                    dve.wait_ge(part_ready, done + 3)

            layer_norm(0)
            layer_norm(1)
            split(0)
            dve.wait_ge(f_loaded, 16 * 5)
            dve.reciprocal(inverse[:], scales[:]).then_inc(factors_ready, 1)
            dve.wait_ge(factors_ready, 1)
            dve.tensor_scalar(half_inverse[:], inverse[:], 0.5, None, ALU.mult).then_inc(factors_ready, 1)
            dve.tensor_tensor(scale_both[:], scales[:, 0:1], scales[:, 1:2], ALU.mult).then_inc(factors_ready, 1)
            split(1)

            CHAIN = NC * NP + 1

            def maxima(G, before=None):
                first = isinstance(G, int) and G == 0

                def split_max(c, k):
                    parts_at = [max_parts[:, c, p * J * TC:(p + 1) * J * TC] for p in range(NP)]
                    if c == 1 or k > 0:
                        dve.wait_ge(max_chain, CHAIN * G + k - NP * c)
                    if k == 0:
                        dve.tensor_copy(parts_at[0], neg_max[:, c, :]).then_inc(max_chain, 1)
                    elif k == 1:
                        dve.tensor_tensor(max_rest[:, c, :], neg_max[:, c, :], parts_at[0], ALU.subtract).then_inc(max_chain, 1)
                    elif k == 2:
                        dve.tensor_copy(parts_at[1], max_rest[:, c, :]).then_inc(max_chain, 1)
                    else:
                        dve.tensor_tensor(parts_at[2], max_rest[:, c, :], parts_at[1], ALU.subtract).then_inc(max_ready, 1)

                def split_last(n):
                    if n == 0:
                        dve.wait_ge(bank_free, NR * G + A_RING)
                        dve.tensor_reduce(neg_max[:, 1, :], part_min[:], AX.X, ALU.min).then_inc(max_chain, 1)
                    elif n <= 2:
                        split_max(1, 2 * n - 2)
                        split_max(1, 2 * n - 1)

                for n, unit in enumerate(RING):
                    if before:
                        before(n)
                    if not first:
                        split_last(n)
                    if C0_LAST + 2 <= n <= C0_LAST + NP + 2:
                        if n == C0_LAST + 2:
                            dve.wait_ge(bank_free, NR * G + C0_LAST + 1 + A_RING)
                        split_max(0, n - C0_LAST - 2)
                    if first and n == TURN_AT[1]:
                        continue
                    if isinstance(G, int) and G == NG and n < TURN_AT[1]:
                        continue
                    count = 1 + (RING_ADD if n == len(RING) - 1 else 0)
                    if first and n == TURN_AT[1] - 1:
                        count += 1
                    if isinstance(G, int) and G == NG:
                        count += n
                    dve.wait_ge(bank_ready, NR * G + n + 1)
                    if unit[0] != TURN and unit[1][0][5]:
                        dve.sem_inc(max_begun, 1)
                    bank = ps_max[:, n % A_RING, :]
                    if unit[0] == TURN:
                        c = unit[1]
                        if not (isinstance(G, int) and G <= c):
                            dve.wait_ge(max_rows[c], 16 * (G - c))
                        dve.tensor_copy(max_turned[:, c, :], turned_view(bank)[0:NP * J * TC]).then_inc(bank_free, count)
                        if isinstance(G, int) and G == NG:
                            return
                        continue
                    for k, (col, j, i, _, blocks, diag, part) in enumerate(unit[1]):
                        src = bank[:, col:col + 128 * blocks]
                        at = j * TC + i % TC
                        to = neg_max[:, 0, at:at + 1] if part is None else part_min[:, at, part:part + 1]
                        if diag:
                            last = dve.tensor_tensor_reduce(
                                out=unused[:, n % UNUSED, k, 0:128 * blocks], in0=src,
                                in1=mask_qk[:, C - 128 * blocks:], scale=-1.0, scalar=-MASKED, op0=ALU.add,
                                op1=ALU.min, accum_out=to)
                        else:
                            last = dve.tensor_reduce(to, src, AX.X, ALU.max, negate=True)
                    last.then_inc(bank_free, count)

            dve.sem_inc(bank_free, A_RING)
            dve.wait_ge(eps_set, 2)
            maxima(0, lambda n: n in LATE_NORMS and layer_norm(NC + LATE_NORMS.index(n)))
            with dve.Fori(0, NLOOP) as it:
                for s in range(2):
                    maxima(2 * it + s + 1)
            maxima(NG - 1)
            maxima(NG)

            fin = 0

            def fin_link(ins):
                nonlocal fin
                fin += 1
                ins.then_inc(fin_chain, 1)
                dve.wait_ge(fin_chain, fin)

            def finish_att(n):
                dve.wait_ge(att_loaded[n], 32)
                fin_link(dve.reciprocal(sums[:, n, :], sums[:, n, :]))
                dve.tensor_tensor(att[:, n, :], att[:, n, :], sums[:, n, :], ALU.mult).then_inc(att_ready, 1)

            def finish_out(n):
                dve.wait_ge(y_ready, n + 1)
                tiles = slice(n * TC, (n + 1) * TC)
                ins = dve.tensor_tensor(y_out[:, n, :, :], ps_max[:, 1 + n % 2, :].rearrange("p (t d) -> p t d", d=D),
                                        xs[:, tiles, :], ALU.add)
                ins.then_inc(y_used, 1)
                dve.wait_ge(y_used, n + 1)
                dve.wait_ge(ffn_done, n + 1)
                dve.tensor_tensor(y_out[:, n, :, :], y_out[:, n, :, :], ffn[:, tiles, :], ALU.add).then_inc(y_out_ready, 1)

            finish_att(0)
            finish_att(1)
            finish_out(0)
            finish_out(1)
            finish_att(2)
            finish_out(2)
            finish_att(3)
            finish_out(3)

        @block.tensor
        def _(pe):
            pe.wait_ge(consts, 1)
            pe.wait_ge(w_loaded, 48)
            def turn_x(n):
                for i in range(TC):
                    pe.wait_ge(xn_ready, n * TC + i + 1)
                    last = pe.transpose(ps[:, TURN_BANKS[n], i * 128:(i + 1) * 128], xn[:, n * TC + i, :], identf[:])
                last.then_inc(turned, 1)

            def project_in(n):
                bq, bk, bv = PREP_BANKS[n]
                pe.wait_ge(xnT_ready, n + 1)
                moving = xnT[:, n * C:(n + 1) * C]
                pe.matmul(ps[:, bq, :], w_qk[:, 0, :], moving, start=True, stop=True).then_inc(q_ready, 1)
                pe.matmul(ps[:, bk, :], w_qk[:, 1, :], moving, start=True, stop=True).then_inc(k_ready, 1)
                if n >= NC:
                    pe.wait_ge(v_copied, n)
                for i in range(TC):
                    last = pe.matmul(ps[:, bv, i * 128:(i + 1) * 128], xnT[:, (n * TC + i) * 128:(n * TC + i + 1) * 128],
                                     w_sb[:, 2, :], start=True, stop=True)
                last.then_inc(v_ready, 1)

            turn_x(0)
            pe.wait_ge(w_turned, 2)
            project_in(0)
            turn_x(1)
            project_in(1)

            def ring_unit(G, s, n):
                unit = RING[n]
                bank = ps_max[:, n % A_RING, :]
                if n == TURN_AT[1] and isinstance(G, int) and G == 0:
                    return
                count = 1 + (RING_ADD if n == len(RING) - 1 else 0)
                if isinstance(G, int) and G == 0 and n == TURN_AT[1] - 1:
                    count += 1
                if isinstance(G, int) and G == NG:
                    count += n
                if unit[0] == TURN:
                    c = unit[1]
                    pe.wait_ge(max_ready, NC * (G - c) + c + 1)
                    pe.wait_ge(bank_free, NR * G + (A_RING if isinstance(G, int) and G == NG else n + 1))
                    pe.transpose(turned_view(bank), max_parts[:, c, :], ident[:]).then_inc(bank_ready, count)
                    return
                c, pieces = unit
                pe.wait_ge(bank_free, NR * G + n + 1)
                for col, j, i, k0, nk, _, _ in pieces:
                    width = nk * 128
                    q0 = (i % TC) * 128
                    last = pe.matmul(bank[:, col:col + width], qr[0:PAD_ROWS, s, i // TC, j, q0:q0 + 128],
                                     kr[0:PAD_ROWS, s, k0 // TC, j, (k0 % TC) * 128:(k0 % TC) * 128 + width],
                                     start=True, stop=True)
                last.then_inc(bank_ready, count)

            def pass_a(G, s, turn, ns):
                for n in ns:
                    if n == 0:
                        pe.wait_ge(rows_loaded[s][0], 16 * 2 * NP * (turn + 1))
                    if n == C1_FIRST:
                        pe.wait_ge(rows_loaded[s][1], 16 * 2 * NP * (turn + 1))
                    ring_unit(G, s, n)

            def scores(G, s, n, step):
                c, pieces = STEPS[step]
                if step == 0 or step == Q0_FREE:
                    pe.wait_ge(max_rows[c], 16 * (G + 1))
                if not (isinstance(n, int) and n < S_RING):
                    pe.wait_ge(probs_ready, n + 1 - S_RING)
                for col, j, kb, q0, width, _ in pieces:
                    to = ps_scores[:, step % S_RING, :]
                    last = pe.matmul(to[:, col:col + width],
                                     kr[0:MAX_ROWS, s, kb // TC, j, (kb % TC) * 128:(kb % TC) * 128 + 128],
                                     qr[0:MAX_ROWS, s, c, j, q0:q0 + width], start=True, stop=True)
                last.then_inc(scores_ready, 1)

            def values(G, s, place, between):
                steps = VALUES.get(place)
                if steps is None:
                    between(0)
                    return
                c = STEPS[steps[0]][0]
                between(0)
                if steps[0] == 0:
                    pe.wait_ge(v_slot_ready, G + 1)
                if steps[0] in (0, Q0_FREE):
                    pe.wait_ge(out_free, NC * G + c + 1)
                if steps[-1] in MASKED_STEPS:
                    pe.wait_ge(probs_masked, len(MASKED_STEPS) * G + MASKED_STEPS.index(steps[-1]) + 1)
                else:
                    pe.wait_ge(probs_ready, NSTEP * G + steps[-1] + 1)
                todo = value_pieces(place)
                for m, (step, (col, j, kb, q0, width, _)) in enumerate(todo):
                    ins = pe.matmul(ps_out[32 * j:32 * j + 32, q0:q0 + width], vr[:, s, kb, j, :],
                                    probs[:, step % P_RING, col:col + width], start=(kb == 0), stop=(kb == TC * c + 2),
                                    skip_group_check=True)
                    if m == len(todo) - 1:
                        if steps[-1] in (Q0_FREE - 1, NSTEP - 1):
                            ins.then_inc(out_ready, 1)
                        else:
                            ins.then_inc(probs_free, len(steps))
                    between(m + 1)

            def group(G, s, turn, following=True, after_next=True, extra=None):
                for place in range(FIRST, NSTEP + FIRST):
                    if place < NSTEP:
                        scores(G, s, NSTEP * G + place, place)
                    elif following:
                        scores(G + 1, 1 - s, NSTEP * (G + 1) + place - NSTEP, place - NSTEP)
                    elif place >= NSTEP + 2:
                        break

                    def between(m):
                        if place < NSTEP + A_FIRST:
                            if following:
                                pass_a(G + 1, 1 - s, turn + s, SPREAD.get((place, m), []))
                        elif after_next:
                            pass_a(G + 2, s, turn + 1, SPREAD.get((place - NSTEP, m), []))
                        elif following and TURN_AT[1] in SPREAD.get((place - NSTEP, m), []):
                            ring_unit(NG, s, TURN_AT[1])

                    if place < NSTEP + 2:
                        values(G, s, place, between)
                    else:
                        values(G + 1, 1 - s, place - NSTEP, between)
                    if extra:
                        extra(place)

            pe.wait_ge(v_copied, 1)
            pe.wait_ge(part_ready, 2 * NP)
            turn_x(2)
            pass_a(0, 0, 0, range(A_PARTS[0]))
            turn_x(3)
            pe.wait_ge(v_copied, NC)
            pe.wait_ge(part_ready, 2 * NC * NP)
            project_in(2)
            pass_a(0, 0, 0, range(A_PARTS[0], A_PARTS[1]))
            pe.wait_ge(xnT_ready, B * NC)
            project_in(3)
            pass_a(0, 0, 0, range(A_PARTS[1], AHEAD))
            pe.wait_ge(v_copied, B * NC)
            rest = [(0, n) for n in range(AHEAD, len(RING))] + [
                (1, n) for n in sorted(n for (place, _), ns in SPREAD.items() if place < FIRST for n in ns)]
            for place in range(FIRST):
                scores(0, 0, place, place)
                for G, n in rest[len(rest) * place // FIRST:len(rest) * (place + 1) // FIRST]:
                    pass_a(G, G, 0, [n])
                values(0, 0, place, lambda m: None)
            with pe.Fori(0, NLOOP) as it:
                for s in range(2):
                    group(2 * it + s, s, it)
            group(NG - 2, 0, NG // 2 - 1, after_next=False)

            def dense(n):
                if n == 0:
                    pe.wait_ge(bank_free, NR * NG + A_RING + TURN_AT[1] + 1)
                    pe.wait_ge(quantised, 1)
                else:
                    pe.wait_ge(ffn_scaled, n)
                for i in range(TC):
                    t = n * TC + i
                    last = pe.matmul(ps_max[:, 0, i * 128:(i + 1) * 128], xq[:, t * 128:(t + 1) * 128], kq[:],
                                     start=True, stop=True)
                last.then_inc(ffn_ready, 1)

            def project(n):
                pe.wait_ge(att_ready, n + 1)
                if n >= 2:
                    pe.wait_ge(y_used, n - 1)
                if n == 0:
                    pe.wait_ge(f_loaded, 16 * 5)
                for i in range(TC):
                    last = pe.matmul(ps_max[:, 1 + n % 2, i * 128:(i + 1) * 128], att[:, n, i * 128:(i + 1) * 128],
                                     w_sb[:, 3, :], start=True, stop=True)
                last.then_inc(y_ready, 1)

            def last_group_extra(place):
                if 7 <= place < 7 + B * NC:
                    dense(place - 7)
                if place == 11:
                    project(0)
                if place == 13:
                    project(1)

            group(NG - 1, 1, NG // 2 - 1, following=False, after_next=False, extra=last_group_extra)
            project(2)
            project(3)


LATE_NORMS = [0, 3]
A_PARTS = [4, 8]
AHEAD = 20
PREP_BANKS = [(4, 5, 6), (7, 0, 1), (0, 1, 2), (3, 7, 2)]
TURN_BANKS = [0, 1, 2, 3]

_INS = ['L0_attn_x', 'L0_attn_WQ', 'L0_attn_WK', 'L0_attn_WV', 'L0_attn_WO', 'L0_ffn_kernel',
        'L0_ffn_input_scale', 'L0_ffn_kernel_scale', 'L0_ffn_bias']


def kernel(**inputs):
    import numpy as _np
    import concourse.bacc as _bacc
    from concourse import mybir as _mybir
    from concourse.bass_utils import run_bass_kernel_spmd as _run

    nc = _bacc.Bacc("TRN2", target_bir_lowering=False, num_devices=1)
    arrays, args = {}, []
    for name in _INS:
        a = _np.ascontiguousarray(inputs[name])
        arrays[f"in_{name}"] = a
        args.append(nc.dram_tensor(f"in_{name}", a.shape, _mybir.dt.from_np(a.dtype), kind="ExternalInput").ap())
    out = nc.dram_tensor("out", (B, S, D), fp32, kind="ExternalOutput").ap()
    attention_kernel(nc, *args, out)
    r = _run(nc, [arrays], core_ids=[0])
    return r.results[0]["out"]
```

```python
import concourse.bass as bass
from concourse import mybir
from contextlib import ExitStack

fp32 = mybir.dt.float32
bf16 = mybir.dt.bfloat16
fp8 = mybir.dt.float8e4
u32 = mybir.dt.uint32
ALU = mybir.AluOpType
ACT = mybir.ActivationFunctionType
AX = mybir.AxisListType

B, S, D = 2, 1024, 128
H = 16
DK = D // H
J = 4
GB = H // J
NG = B * GB
T = S // 128
C = 512
NC = S // C
TC = C // 128
NP = 3
SPLIT_ROWS = NP * NP * DK
PAD_ROWS = 96
MAX_ROWS = PAD_ROWS + NP
VW = 32
MASKED = -3.0e38
EPS = 1e-5
SCALE = float(DK) ** -0.5
BF16_ONES = 1.0019378662109375
FP8_TOP = 240.0
OVERFLOW = 7.3e35
P_RING = 6
FX = B * S // NG
FIRST = 4
A_FIRST = 0
S_RING = 2
A_RING = 3
UNUSED = A_RING + 1
PV_COST = 1.25
TURN_COST = 600
SPAN = 0.96


def score_steps():
    steps = []
    for c in range(NC):
        first = TC * c
        for kb in range(first + 1):
            for pair in range(2):
                steps.append((c, [(C * n, 2 * pair + n, kb, 0, C, kb == first) for n in range(2)]))
        for pair in range(2):
            steps.append((c, [p for n in range(2) for p in (
                (C * n, 2 * pair + n, first + 1, 128, 384, True),
                (C * n + 384, 2 * pair + n, first + 3, 384, 128, True))]))
        steps.append((c, [(256 * j, j, first + 2, 256, 256, True) for j in range(J)]))
    return steps


def max_units():
    units = []
    for pair in (0, 2):
        for j in (pair, pair + 1):
            units.append((0, [(0, j, 3, 0, 4, True, None)]))
        for j in (pair, pair + 1):
            units.append((0, [(0, j, 2, 0, 3, True, None), (384, j, 0, 0, 1, True, None)]))
        units.append((0, [(256 * n, pair + n, 1, 0, 2, True, None) for n in range(2)]))
    for pair in (0, 2):
        for j in (pair, pair + 1):
            for i in range(4, 8):
                units.append((1, [(0, j, i, 0, 4, False, 0)]))
            units.append((1, [(0, j, 7, 4, 4, True, 1)]))
            units.append((1, [(0, j, 6, 4, 3, True, 1), (384, j, 4, 4, 1, True, 1)]))
        units.append((1, [(256 * n, pair + n, 5, 4, 2, True, 1) for n in range(2)]))
    return units


STEPS = score_steps()
MASKED_STEPS = [n for n, (_, pieces) in enumerate(STEPS) if pieces[0][5]]
NSTEP = len(STEPS)
UNITS = max_units()
N0 = sum(c == 0 for c, _ in UNITS)
TURN = "turn"
RING = UNITS[:4] + [(TURN, 1)] + UNITS[4:N0 + NP + 3] + [(TURN, 0)] + UNITS[N0 + NP + 3:]
TURN_AT = [RING.index((TURN, c)) for c in range(NC)]
C0_LAST, C1_FIRST = RING.index(UNITS[N0 - 1]), RING.index(UNITS[N0])
RING_ADD = -len(RING) % A_RING
NR = len(RING) + RING_ADD
Q0_FREE = sum(c == 0 for c, _ in STEPS)
K0_FREE = Q0_FREE + 2 * TC
VALUES = {}
_s = 0
while _s < NSTEP:
    _n = 1 if _s + 1 == NSTEP or STEPS[_s + 1][0] != STEPS[_s][0] else 2
    VALUES[_s + _n - 1 + 2] = list(range(_s, _s + _n))
    _s += _n
O0_DONE = Q0_FREE - 1 + 2


def values_place(place):
    return place % NSTEP + (NSTEP if place % NSTEP < 2 else 0)


def value_pieces(place):
    return sorted(((step, p) for step in VALUES.get(place, []) for p in STEPS[step][1]),
                  key=lambda e: (e[1][2], e[0], e[1][1]))


def spread_units():
    spots, at = [], 0
    for place in range(A_FIRST, NSTEP + A_FIRST):
        at += sum(piece[4] for piece in STEPS[place % NSTEP][1])
        spots.append((at, (place, 0)))
        for m, (_, piece) in enumerate(value_pieces(values_place(place))):
            at += piece[4] * PV_COST
            spots.append((at, (place, m + 1)))
    need = [TURN_COST if unit[0] == TURN else sum(128 * p[4] + 96 for p in unit[1]) for unit in RING]
    where, spent = {}, 0
    for n in range(len(RING)):
        due = at * SPAN * spent / sum(need)
        where.setdefault(min(spot for spot in spots if spot[0] >= due)[1], []).append(n)
        spent += need[n]
    return where


SPREAD = spread_units()

TURN_BANKS = [0, 1, 2, 3]
PREP_BANKS = [(4, 5, 6), (7, 0, 1), (0, 1, 2), (3, 7, 2)]
LATE_NORMS = [0, 3]
A_BEFORE = [4, 2, 6]
AHEAD = 26
KEEP_FIRST, KEEP_LATE = 20, 20

DENSE_PLACES = [6, 7, 8, 9]
LAST = B * NC - 1
LAST_ROWS = J * DK * (GB - 1)
ENDS = [(0, 0, TC), (1, 0, TC), (LAST, 0, TC // 2), (2, 0, TC), (LAST, TC // 2, TC // 2)]
HALVES = [2, 4]
ATT_ORDER = [1, 2, 5, 4, 6]
END_BANKS = [5, 6, 0, 1, 2]


def attention_kernel(nc, x, wq, wk, wv, wo, wf, s_in, s_k, bias, out):
    ctx = ExitStack()
    with ctx:
        def sb(name, shape, dt):
            return ctx.enter_context(nc.sbuf_tensor(name, shape, dt))

        def sem(name):
            return ctx.enter_context(nc.semaphore(name))

        parts_dram = nc.dram_tensor("parts_dram", (2, NC, NG, DK, NP, J, C), bf16, kind="Internal").ap()
        raw_dram = nc.dram_tensor("raw_dram", (NG, 128, S), fp32, kind="Internal").ap()

        xs = sb("xs", [128, B * T, D], fp32)
        xn = sb("xn", [128, B * T, D], fp32)
        stats = sb("stats", [128, B * T, 6], fp32)
        moments = sb("moments", [128, B * T, 2], fp32)
        std = sb("std", [128, B * T], fp32)
        rstd = sb("rstd", [128, B * T], fp32)
        eps = sb("eps", [128, 1], fp32)
        warm = sb("warm", [128, 1], fp32)
        w_sb = sb("w_sb", [128, 4, D], fp32)
        w_qk = sb("w_qk", [128, 2, D], fp32)
        wf_sb = sb("wf_sb", [128, D], bf16)
        bias_sb = sb("bias_sb", [128, D], bf16)
        scales = sb("scales", [128, 2], fp32)
        inverse = sb("inverse", [128, 2], fp32)
        half_inverse = sb("half_inverse", [128, 2], fp32)
        scale_both = sb("scale_both", [128, 1], fp32)
        identf = sb("identf", [128, 128], fp32)
        ident = sb("ident", [128, 128], bf16)
        mask_qk = sb("mask_qk", [128, C], bf16)
        xnT = sb("xnT", [128, B * S], fp32)
        parts = sb("parts", [128, 2, NP, B * S], bf16)
        rest = sb("rest", [128, 2, C], fp32)
        qk1 = sb("qk1", [128, 2, S], fp32)
        v_all = sb("v_all", [128, NG, T, 32], fp32)
        xq = sb("xq", [128, B * S], bf16)
        kq = sb("kq", [128, D], bf16)
        f_x = sb("f_x", [128, FX], bf16)
        f_a = sb("f_a", [128, FX], fp32)
        f_b = sb("f_b", [128, FX], fp32)
        f_c = sb("f_c", [128, FX], fp32)
        f8_big = sb("f8_big", [128, FX], fp8)
        f8_small = sb("f8_small", [128, FX], fp8)

        qr = sb("qr", [128, 2, NC, J, C], bf16)
        kr = sb("kr", [128, 2, NC, J, C], bf16)
        vr = sb("vr", [128, 2, T, J, VW], fp32)
        probs = sb("probs", [128, P_RING, 2 * C], fp32)
        part_min = sb("part_min", [128, J * TC, 2], fp32)
        unused = sb("unused", [128, UNUSED, 2, C], bf16)
        neg_max = sb("neg_max", [128, NC, J * TC], fp32)
        max_rest = sb("max_rest", [128, NC, J * TC], fp32)
        max_parts = sb("max_parts", [128, NC, 128], bf16)
        max_turned = sb("max_turned", [NP * J * TC, NC, 128], bf16)
        raw_sb = sb("raw_sb", [128, NC, C], fp32)
        att = sb("att", [128, NC * B, C], fp32)
        sums = sb("sums", [128, NC * B, C], fp32)
        att_last = sb("att_last", [128, C], fp32)
        sums_last = sb("sums_last", [128, C], fp32)
        wo_last = sb("wo_last", [128, D], fp32)
        spread = sb("spread", [128, 128], fp32)
        y_sb = sb("y_sb", [128, NC * B, TC, D], bf16)
        ffn = sb("ffn", [128, B * T, D], bf16)
        y_out = sb("y_out", [128, NC * B, TC, D], fp32)

        ps = ctx.enter_context(nc.psum_tensor("ps", [128, 8, C], fp32))
        ps_scores = ps[:, 0:4, :].rearrange("p (s b) c -> p s (b c)", s=S_RING)
        ps_max = ps[:, 4:7, :]
        ps_out = ps[:, 7, :]

        x_loaded = [sem(f"x_loaded{n}") for n in range(B * NC)]
        w_loaded = sem("w_loaded")
        f_loaded = sem("f_loaded")
        w_turned = sem("w_turned")
        consts_zero = sem("consts_zero")
        consts = sem("consts")
        rows_set = sem("rows_set")
        norm = sem("norm")
        std_ready = sem("std_ready")
        eps_set = sem("eps_set")
        table_loaded = sem("table_loaded")
        xn_ready = sem("xn_ready")
        turned = sem("turned")
        xnT_ready = sem("xnT_ready")
        q_ready = sem("q_ready")
        k_ready = sem("k_ready")
        v_ready = sem("v_ready")
        hi_ready = sem("hi_ready")
        v_copied = sem("v_copied")
        qk1_ready = sem("qk1_ready")
        prep_chain = sem("prep_chain")
        rest_ready = sem("rest_ready")
        mid_ready = sem("mid_ready")
        lo_ready = sem("lo_ready")
        rest1_ready = sem("rest1_ready")
        middle_ready = sem("middle_ready")
        low_ready = sem("low_ready")
        stored = [[sem(f"{t}_stored{c}") for t in "qk"] for c in range(NC)]
        row1_stored = sem("row1_stored")
        rows_loaded = [[sem(f"rows_loaded{s}{c}") for c in range(NC)] for s in range(2)]
        v_slot_ready = sem("v_slot_ready")
        scores_ready = sem("scores_ready")
        probs_ready = sem("probs_ready")
        probs_masked = sem("probs_masked")
        mask_begun = sem("mask_begun")
        max_begun = sem("max_begun")
        probs_free = sem("probs_free")
        out_ready = sem("out_ready")
        out_free = sem("out_free")
        raw_stored = [sem(f"raw_stored{c}") for c in range(NC)]
        bank_ready = sem("bank_ready")
        bank_free = sem("bank_free")
        max_ready = sem("max_ready")
        max_chain = sem("max_chain")
        max_rows = [sem(f"max_rows{c}") for c in range(NC)]
        factors_ready = sem("factors_ready")
        quantised = sem("quantised")
        ffn_ready = sem("ffn_ready")
        ffn_scaled = sem("ffn_scaled")
        ffn_done = sem("ffn_done")
        att_loaded = [sem(f"att_loaded{n}") for n in range(B * NC)]
        att_ready = sem("att_ready")
        wo_loaded = sem("wo_loaded")
        last_set = sem("last_set")
        sums_ready = sem("sums_ready")
        fin_chain = sem("fin_chain")
        y_ready = sem("y_ready")
        x_ffn_ready = [sem(f"x_ffn_ready{b}") for b in range(B)]
        y_out_ready = sem("y_out_ready")
        out_stored = sem("out_stored")

        block = ctx.enter_context(nc.Block())

        x_tiles = x.rearrange("b (t p) d -> b p t d", p=128)
        out_tiles = out.rearrange("b (t p) d -> b p t d", p=128)
        NLOOP = (NG - 2) // 2

        def turned_view(bank):
            return bank[:, 0:64].bitcast(bf16)

        def store_part(eng, t, b, c, p, done):
            eng.dma_start(parts_dram[t, c, b * GB:(b + 1) * GB, :, p, :, :].rearrange("g d j t -> (g d) j t"),
                          parts[:, t, p, b * S + c * C:b * S + (c + 1) * C]).then_inc(done, 16)

        @block.sync
        def _(sp):
            for n in range(B * NC):
                sp.dma_start(xs[:, n * TC:(n + 1) * TC, :], x_tiles[n // NC][:, (n % NC) * TC:(n % NC + 1) * TC, :]
                             ).then_inc(x_loaded[n], 16)
                if n == 0:
                    for m, w in enumerate((wq, wk, wv)):
                        sp.dma_start(w_sb[:, m, :], w).then_inc(w_loaded, 16)
            for n, w in enumerate((s_in, s_k)):
                sp.dma_start(scales[:, n:n + 1], w.rearrange("(a n) -> a n", a=1).broadcast_to([128, 1])).then_inc(f_loaded, 16)
            sp.dma_start(bias_sb[:], bias.rearrange("(a n) -> a n", a=1).broadcast_to([128, D])).then_inc(f_loaded, 16)
            sp.dma_start(wf_sb[:], wf).then_inc(f_loaded, 16)
            sp.dma_start(w_sb[:, 3, :], wo).then_inc(f_loaded, 16)

            def load_rows(G, s, c, what):
                if "q" in what:
                    sp.dma_start(qr[0:SPLIT_ROWS, s, c, :, :].rearrange("a j t -> a (j t)"),
                                 parts_dram[0, c, G].rearrange("d p j t -> (d p) (j t)").unsqueeze(0)
                                 .broadcast_to([NP, NP * DK, J * C])).then_inc(rows_loaded[s][c], 16)
                if "k" in what:
                    for r in range(NP):
                        sp.dma_start(kr[NP * DK * r:NP * DK * (r + 1), s, c, :, :].rearrange("a j t -> a (j t)"),
                                     parts_dram[1, c, G, :, r].rearrange("d j t -> d (j t)").unsqueeze(1)
                                     .broadcast_to([DK, NP, J * C])).then_inc(rows_loaded[s][c], 16)

            def store_raw(G, c, done):
                sp.wait_ge(out_free, done + 1)
                sp.dma_start(raw_dram[G, :, c * C:(c + 1) * C], raw_sb[:, c, :]).then_inc(raw_stored[c], 16)

            def store_max_rows(G, s, c):
                sp.wait_ge(bank_free, A_RING + NR * (G + c) + TURN_AT[c] + 1)
                sp.dma_start(qr[PAD_ROWS:PAD_ROWS + NP, s, c, :, :].rearrange("p j t -> p (j t)"),
                             max_turned[:, c, :]).then_inc(max_rows[c], 16)

            def group(G, s, loads, maxima):
                if loads:
                    sp.wait_ge(scores_ready, NSTEP * G + Q0_FREE)
                    load_rows(G + 2, s, 0, "q")
                store_raw(G, 0, NC * G + 1)
                if maxima:
                    store_max_rows(G + 1, 1 - s, 0)
                if loads:
                    sp.wait_ge(scores_ready, NSTEP * G + K0_FREE)
                    load_rows(G + 2, s, 0, "k")
                if loads:
                    sp.wait_ge(scores_ready, NSTEP * (G + 1))
                    load_rows(G + 2, s, 1, "qk")
                store_raw(G, 1, NC * G + 2)
                if maxima:
                    store_max_rows(G + 1, 1 - s, 1)

            for p, t in ((0, 0), (0, 1), (1, 0), (2, 0), (1, 1), (2, 1)):
                sp.wait_ge((hi_ready, mid_ready, lo_ready)[p], t + 1)
                store_part(sp, t, 0, 0, p, stored[0][t])
            sp.wait_ge(rows_set, 2)
            for c in range(NC):
                for t in range(2):
                    sp.wait_ge(stored[c][t], 16 * NP)
                    load_rows(0, 0, c, "qk"[t])
            for c in range(NC):
                load_rows(1, 1, c, "qk")
            store_max_rows(0, 0, 0)
            for t in range(2):
                for p in range(NP):
                    if p < 2:
                        sp.wait_ge((qk1_ready, middle_ready)[p], (2 * (NC - 1) + t + 1, t + 1)[p])
                    else:
                        sp.wait_ge(low_ready, t + 1)
                    for c in range(NC):
                        store_part(sp, t, 1, c, p, row1_stored)
            store_max_rows(0, 0, 1)
            sp.wait_ge(row1_stored, 16 * 2 * NP * NC)

            def load_att(n):
                b, c = divmod(n, NC)
                groups = GB - (1 if n == LAST else 0)
                sp.wait_ge(raw_stored[c], 16 * (b * GB + groups + 1))
                src = raw_dram[b * GB:b * GB + groups, :, c * C:(c + 1) * C].rearrange("g (j r) t -> (g j) r t", j=J)
                rows = J * DK * groups
                sp.dma_start(att[0:rows, n, :], src[:, 0:DK, :]).then_inc(att_loaded[n], 16)
                sp.dma_start(sums[0:rows, n, :], src[:, DK:2 * DK, :]).then_inc(att_loaded[n], 16)

            def store_out(m):
                n, i, blocks = ENDS[m]
                b, c = divmod(n, NC)
                sp.wait_ge(y_out_ready, m + 1)
                sp.dma_start(out_tiles[b, :, c * TC + i:c * TC + i + blocks, :], y_out[:, n, i:i + blocks, :]
                             ).then_inc(out_stored, 16)

            with sp.Fori(0, NLOOP) as it:
                for s in range(2):
                    group(2 * it + s, s, True, True)
            load_att(0)
            load_att(1)
            sp.wait_ge(last_set, 2)
            for j in range(J):
                sp.dma_start(wo_last[32 * j:32 * j + DK, :], wo[LAST_ROWS + j * DK:LAST_ROWS + (j + 1) * DK, :]
                             ).then_inc(wo_loaded, 16)
            group(NG - 2, 0, False, True)
            load_att(LAST)
            store_raw(NG - 1, 0, NC * (NG - 1) + 1)
            load_att(2)
            for m in range(len(ENDS)):
                store_out(m)
            sp.wait_ge(out_stored, 16 * len(ENDS))

        @block.gpsimd
        def _(pool):
            pool.memset(identf[:], 0.0).then_inc(consts_zero, 1)
            pool.wait_ge(consts_zero, 1)
            pool.affine_select(out=identf[:], in_=identf[:], compare_op=ALU.not_equal, fill=1.0, base=0,
                               pattern=[[-1, 128]], channel_multiplier=1).then_inc(consts, 1)
            pool.memset(mask_qk[:], 0.0).then_inc(consts_zero, 1)
            pool.wait_ge(consts_zero, 2)
            pool.affine_select(out=mask_qk[:, C - 128:], in_=mask_qk[:, C - 128:], compare_op=ALU.is_ge, fill=MASKED,
                               base=0, pattern=[[-1, 128]], channel_multiplier=1).then_inc(consts, 1)
            pool.wait_ge(consts, 1)
            pool.tensor_copy(ident[:], identf[:]).then_inc(consts, 1)
            pool.wait_ge(consts, 3)
            pool.memset(kr[64:128].rearrange("p s c j t -> p (s c j t)").bitcast(fp32), BF16_ONES).then_inc(rows_set, 1)
            pool.wait_ge(rows_set, 1)
            pool.memset(qr[64:PAD_ROWS].rearrange("p s c j t -> p (s c j t)").bitcast(u32), 0).then_inc(rows_set, 1)
            pool.wait_ge(rows_set, 2)
            pool.memset(vr[:], 1.0).then_inc(rows_set, 1)
            def quantise(src, dst, n):
                w = src.shape[1]
                pool.tensor_scalar(f_a[:, 0:w], src, half_inverse[:, n:n + 1], FP8_TOP, ALU.mult, ALU.min)
                pool.drain()
                pool.tensor_scalar(f_a[:, 0:w], f_a[:, 0:w], -FP8_TOP, None, ALU.max)
                pool.drain()
                pool.tensor_copy(f8_big[:, 0:w], f_a[:, 0:w], saturate=False)
                pool.drain()
                pool.tensor_copy(f_c[:, 0:w], f8_big[:, 0:w])
                pool.drain()
                pool.tensor_scalar(f_b[:, 0:w], f_c[:, 0:w], -0.5, 0.5, ALU.max, ALU.min)
                pool.drain()
                pool.tensor_tensor(f_c[:, 0:w], f_c[:, 0:w], f_b[:, 0:w], ALU.subtract)
                pool.drain()
                pool.tensor_scalar(f_c[:, 0:w], f_c[:, 0:w], 2.0, None, ALU.mult)
                pool.drain()
                pool.tensor_scalar(f_a[:, 0:w], src, inverse[:, n:n + 1], 1.0, ALU.mult, ALU.min)
                pool.drain()
                pool.tensor_scalar(f_a[:, 0:w], f_a[:, 0:w], -1.0, None, ALU.max)
                pool.drain()
                pool.tensor_copy(f8_small[:, 0:w], f_a[:, 0:w], saturate=False)
                pool.drain()
                pool.tensor_tensor(f_c[:, 0:w], f_c[:, 0:w], f8_small[:, 0:w], ALU.add)
                pool.drain()
                pool.tensor_scalar(f_a[:, 0:w], f_c[:, 0:w], OVERFLOW, 0.0, ALU.mult, ALU.mult)
                pool.drain()
                return pool.tensor_tensor(dst, f_c[:, 0:w], f_a[:, 0:w], ALU.add)

            pool.wait_ge(f_loaded, 16 * 5)
            pool.wait_ge(factors_ready, 3)
            quantise(wf_sb[:], kq[:], 1)

            for t in range(2):
                for p in range(NP):
                    pool.wait_ge((hi_ready, mid_ready, lo_ready)[p], 2 + t + 1)
                    store_part(pool, t, 0, 1, p, stored[1][t])

            def quantise_share(n):
                pool.tensor_copy(f_x[:], xnT[:, bass.ts(n, FX)])
                pool.drain()
                return quantise(f_x[:], xq[:, bass.ts(n, FX)], 0)

            quantise_share(0)

            for t in range(2):
                pool.wait_ge(qk1_ready, 2 * (NC - 1) + t + 1)
                pool.tensor_tensor(qk1[:, t, :], qk1[:, t, :], parts[:, t, 0, S:2 * S], ALU.subtract).then_inc(rest1_ready, 1)
            for t in range(2):
                pool.wait_ge(middle_ready, t + 1)
                pool.tensor_tensor(parts[:, t, 2, S:2 * S], qk1[:, t, :], parts[:, t, 1, S:2 * S], ALU.subtract
                                   ).then_inc(low_ready, 1)

            def mask_probs(G, step):
                c, pieces = STEPS[step]
                blocks = probs[:, step % P_RING, :]
                if len(pieces) == 2:
                    views = [blocks.rearrange("p (a b) -> p a b", a=2)[:, :, 0:128]]
                elif pieces[1][0] == 384:
                    views = [half.rearrange("p (a b) -> p a b", b=128)[:, 0:4:3, :] for half in (blocks[:, 0:C], blocks[:, C:2 * C])]
                else:
                    views = [blocks.rearrange("p (a b) -> p a b", a=4)[:, :, 0:128]]
                pool.wait_ge(probs_ready, NSTEP * G + step + 1)
                pool.sem_inc(mask_begun, 1)
                for view in views:
                    last = pool.affine_select(out=view, in_=view, compare_op=ALU.is_ge, fill=0.0, base=0,
                                              pattern=[[0, view.shape[1]], [1, 128]], channel_multiplier=-1)
                last.then_inc(probs_masked, 1)

            def add_bias(n):
                tiles = slice(n * TC, (n + 1) * TC)
                pool.wait_ge(ffn_scaled, n + 1)
                pool.tensor_tensor(ffn[:, tiles, :], y_sb[:, n, :, :],
                                   bias_sb[:, :].unsqueeze(1).broadcast_to([128, TC, D]), ALU.add).then_inc(ffn_done, 1)

            def group(G, final_share=False, last=False):
                for step in MASKED_STEPS:
                    if step >= FIRST:
                        mask_probs(G, step)
                    if step == Q0_FREE - 1:
                        if not last:
                            done = quantise_share(G + 1)
                            if final_share:
                                done.then_inc(quantised, 1)
                        else:
                            for n in range(B * NC):
                                add_bias(n)
                if not last:
                    for step in range(FIRST):
                        mask_probs(G + 1, step)

            pool.memset(wo_last[:], 0.0).then_inc(last_set, 1)
            pool.memset(spread[:], 0.0).then_inc(last_set, 1)
            pool.wait_ge(last_set, 2)
            pool.affine_select(out=spread[:].rearrange("p (j r) -> p j r", j=J), in_=spread[:].rearrange("p (j r) -> p j r", j=J),
                               compare_op=ALU.not_equal, fill=1.0, base=-DK, pattern=[[-32, J], [0, 128 // J]],
                               channel_multiplier=1).then_inc(last_set, 1)
            for step in range(FIRST):
                mask_probs(0, step)
            with pool.Fori(0, NLOOP) as it:
                for s in range(2):
                    group(2 * it + s)
            group(NG - 2, final_share=True)
            group(NG - 1, last=True)
            for n in range(NC, B * NC):
                tiles = slice(n * TC, (n + 1) * TC)
                pool.wait_ge(ffn_done, n + 1)
                pool.tensor_tensor(y_out[:, n, :, :], xs[:, tiles, :], ffn[:, tiles, :], ALU.add).then_inc(x_ffn_ready[1], 1)

        @block.scalar
        def _(act):
            def take_std(n):
                act.wait_ge(norm, n + 1)
                act.activation(std[:, n * TC:(n + 1) * TC], moments[:, n * TC:(n + 1) * TC, 1], ACT.Sqrt,
                               bias=eps[:, 0:1]).then_inc(std_ready, 1)

            def take_xnT(n):
                act.wait_ge(turned, n + 1)
                act.activation(xnT[:, n * C:(n + 1) * C], ps[:, TURN_BANKS[n], :], ACT.Copy).then_inc(xnT_ready, 1)

            def take_qk(n):
                for t, ready in enumerate((q_ready, k_ready)):
                    bank = ps[:, PREP_BANKS[n][t], :]
                    act.wait_ge(ready, n + 1)
                    hi = act.activation(parts[:, t, 0, n * C:(n + 1) * C], bank, ACT.Copy)
                    if n < NC:
                        hi.then_inc(hi_ready, 1)
                    else:
                        act.activation(qk1[:, t, (n - NC) * C:(n - NC + 1) * C], bank, ACT.Copy).then_inc(qk1_ready, 1)

            def take_mid(c, t):
                act.wait_ge(rest_ready, 2 * c + t + 1)
                act.activation(parts[:, t, 1, c * C:(c + 1) * C], rest[:, t, :], ACT.Copy).then_inc(mid_ready, 1)

            def take_v(n):
                b, c = divmod(n, NC)
                act.wait_ge(v_ready, n + 1)
                act.activation(v_all[:, b * GB:(b + 1) * GB, c * TC:(c + 1) * TC, :],
                               ps[:, PREP_BANKS[n][2], :].rearrange("p (t g e) -> p g t e", t=TC, g=GB), ACT.Copy
                               ).then_inc(v_copied, 1)

            act.wait_ge(eps_set, 1)
            act.activation(warm[:], eps[:], ACT.Sqrt).then_inc(table_loaded, 1)
            act.wait_ge(table_loaded, 1)
            take_std(0)
            act.wait_ge(w_loaded, 48)
            for n in range(2):
                act.activation(w_qk[:, n, :].rearrange("p (g d j) -> p g d j", g=GB, j=J),
                               w_sb[:, n, :].rearrange("p (g j d) -> p g d j", g=GB, j=J), ACT.Copy).then_inc(w_turned, 1)
            take_xnT(0)
            take_std(1)
            take_qk(0)
            take_mid(0, 0)
            take_mid(0, 1)
            take_xnT(1)
            take_v(0)
            take_qk(1)
            take_mid(1, 0)
            take_mid(1, 1)
            take_v(1)
            take_std(2)
            take_xnT(2)
            take_std(3)
            act.activation(warm[:], eps[:], ACT.Exp)
            take_xnT(3)
            for n in (2, 3):
                take_qk(n)
                take_v(n)
            for t in range(2):
                act.wait_ge(rest1_ready, t + 1)
                act.activation(parts[:, t, 1, S:2 * S], qk1[:, t, :], ACT.Copy).then_inc(middle_ready, 1)

            def exp_step(G, n, step):
                act.wait_ge(scores_ready, n + 1)
                act.wait_ge(probs_free, n + 1)
                act.activation(probs[:, step % P_RING, :], ps_scores[:, step % S_RING, :], ACT.Exp,
                               scale=SCALE).then_inc(probs_ready, 1)

            def copy_v(G, s):
                act.activation(vr[:, s, :, :, 0:DK],
                               v_all[:, G, :, :].rearrange("p t (j d) -> p t j d", j=J), ACT.Copy).then_inc(v_slot_ready, 1)

            def copy_out(G, c):
                act.wait_ge(out_ready, NC * G + c + 1)
                act.sem_inc(probs_free, 1)
                act.wait_ge(raw_stored[c], 16 * (G + 1))
                act.activation(raw_sb[:, c, :], ps_out, ACT.Copy).then_inc(out_free, 1)

            def group(G, s, last=False):
                for step in range(FIRST, NSTEP):
                    exp_step(G, NSTEP * G + step, step)
                    if step == 4 and not last:
                        act.wait_ge(probs_free, NSTEP * G + P_RING)
                        copy_v(G + 1, 1 - s)
                    if step == O0_DONE:
                        copy_out(G, 0)
                if not last:
                    for step in range(FIRST):
                        exp_step(G, NSTEP * (G + 1) + step, step)
                        if step == 1:
                            copy_out(G, 1)

            act.wait_ge(v_copied, 2)
            act.wait_ge(rows_set, 3)
            copy_v(0, 0)
            act.sem_inc(probs_free, P_RING)
            act.sem_inc(out_free, 1)
            act.sem_inc(raw_stored[0], 16)
            act.sem_inc(raw_stored[1], 16)
            for step in range(FIRST):
                exp_step(0, step, step)
            with act.Fori(0, NLOOP) as it:
                for s in range(2):
                    group(2 * it + s, s)
            group(NG - 2, 0)
            for step in range(FIRST, NSTEP):
                exp_step(NG - 1, NSTEP * (NG - 1) + step, step)
                if step == O0_DONE:
                    copy_out(NG - 1, 0)
            copy_out(NG - 1, 1)

        @block.vector
        def _(dve):
            dve.memset(eps[:], EPS).then_inc(eps_set, 1)
            dve.memset(max_parts[:], 0.0).then_inc(eps_set, 1)
            chain = 0

            def link(ins):
                nonlocal chain
                chain += 1
                ins.then_inc(prep_chain, 1)
                dve.wait_ge(prep_chain, chain)

            def layer_norm(n):
                dve.wait_ge(x_loaded[n], 16)
                tiles = range(n * TC, (n + 1) * TC)
                for t in tiles:
                    last = dve.bn_stats(stats[:, t, :], xs[:, t, :])
                link(last)
                for t in tiles:
                    last = dve.bn_aggr(moments[:, t, :], stats[:, t, :])
                last.then_inc(norm, 1)
                dve.wait_ge(std_ready, n + 1)
                link(dve.reciprocal(rstd[:, n * TC:(n + 1) * TC], std[:, n * TC:(n + 1) * TC]))
                for t in tiles:
                    dve.tensor_scalar(xn[:, t, :], xs[:, t, :], moments[:, t, 0:1], rstd[:, t:t + 1],
                                      ALU.subtract, ALU.mult).then_inc(xn_ready, 1)

            def split(c):
                cols = slice(c * C, (c + 1) * C)
                for t in range(2):
                    dve.wait_ge(hi_ready, 2 * c + t + 1)
                    dve.tensor_tensor(rest[:, t, :], ps[:, PREP_BANKS[c][t], :], parts[:, t, 0, cols], ALU.subtract
                                      ).then_inc(rest_ready, 1)
                for t in range(2):
                    dve.wait_ge(mid_ready, 2 * c + t + 1)
                    dve.tensor_tensor(parts[:, t, 2, cols], rest[:, t, :], parts[:, t, 1, cols], ALU.subtract).then_inc(lo_ready, 1)
                dve.wait_ge(lo_ready, 2 * c + 2)

            layer_norm(0)
            layer_norm(1)
            dve.wait_ge(f_loaded, 16 * 5)
            dve.reciprocal(inverse[:], scales[:]).then_inc(factors_ready, 1)
            dve.wait_ge(factors_ready, 1)
            dve.tensor_scalar(half_inverse[:], inverse[:], 0.5, None, ALU.mult).then_inc(factors_ready, 1)
            dve.tensor_tensor(scale_both[:], scales[:, 0:1], scales[:, 1:2], ALU.mult).then_inc(factors_ready, 1)
            split(0)
            split(1)

            CHAIN = NC * NP + 1

            def maxima(G, before=None):
                first = isinstance(G, int) and G == 0

                def split_max(c, k):
                    parts_at = [max_parts[:, c, p * J * TC:(p + 1) * J * TC] for p in range(NP)]
                    if c == 1 or k > 0:
                        dve.wait_ge(max_chain, CHAIN * G + k - NP * c)
                    if k == 0:
                        dve.tensor_copy(parts_at[0], neg_max[:, c, :]).then_inc(max_chain, 1)
                    elif k == 1:
                        dve.tensor_tensor(max_rest[:, c, :], neg_max[:, c, :], parts_at[0], ALU.subtract).then_inc(max_chain, 1)
                    elif k == 2:
                        dve.tensor_copy(parts_at[1], max_rest[:, c, :]).then_inc(max_chain, 1)
                    else:
                        dve.tensor_tensor(parts_at[2], max_rest[:, c, :], parts_at[1], ALU.subtract).then_inc(max_ready, 1)

                def split_last(n):
                    if n == 0:
                        dve.wait_ge(bank_free, NR * G + A_RING)
                        dve.tensor_reduce(neg_max[:, 1, :], part_min[:], AX.X, ALU.min).then_inc(max_chain, 1)
                    elif n <= 2:
                        split_max(1, 2 * n - 2)
                        split_max(1, 2 * n - 1)

                for n, unit in enumerate(RING):
                    if before:
                        before(n)
                    if not first:
                        split_last(n)
                    if C0_LAST + 2 <= n <= C0_LAST + NP + 2:
                        if n == C0_LAST + 2:
                            dve.wait_ge(bank_free, NR * G + C0_LAST + 1 + A_RING)
                        split_max(0, n - C0_LAST - 2)
                    if first and n == TURN_AT[1]:
                        continue
                    if isinstance(G, int) and G == NG and n < TURN_AT[1]:
                        continue
                    count = 1 + (RING_ADD if n == len(RING) - 1 else 0)
                    if first and n == TURN_AT[1] - 1:
                        count += 1
                    if isinstance(G, int) and G == NG:
                        count += n
                    dve.wait_ge(bank_ready, NR * G + n + 1)
                    if unit[0] != TURN and unit[1][0][5]:
                        dve.sem_inc(max_begun, 1)
                    bank = ps_max[:, n % A_RING, :]
                    if unit[0] == TURN:
                        c = unit[1]
                        dve.wait_ge(max_rows[c], 16 * (G - c + 1))
                        dve.tensor_copy(max_turned[:, c, :], turned_view(bank)[0:NP * J * TC]).then_inc(bank_free, count)
                        if isinstance(G, int) and G == NG:
                            return
                        continue
                    for k, (col, j, i, _, blocks, diag, part) in enumerate(unit[1]):
                        src = bank[:, col:col + 128 * blocks]
                        at = j * TC + i % TC
                        to = neg_max[:, 0, at:at + 1] if part is None else part_min[:, at, part:part + 1]
                        if diag:
                            last = dve.tensor_tensor_reduce(
                                out=unused[:, n % UNUSED, k, 0:128 * blocks], in0=src,
                                in1=mask_qk[:, C - 128 * blocks:], scale=-1.0, scalar=-MASKED, op0=ALU.add,
                                op1=ALU.min, accum_out=to)
                        else:
                            last = dve.tensor_reduce(to, src, AX.X, ALU.max, negate=True)
                    last.then_inc(bank_free, count)

            dve.sem_inc(bank_free, A_RING)
            for c in range(NC):
                dve.sem_inc(max_rows[c], 16)
            dve.wait_ge(eps_set, 2)
            maxima(0, lambda n: n in LATE_NORMS and layer_norm(NC + LATE_NORMS.index(n)))
            with dve.Fori(0, NLOOP) as it:
                for s in range(2):
                    maxima(2 * it + s + 1)
            maxima(NG - 1)
            maxima(NG)

            fin = 0

            def fin_link(ins):
                nonlocal fin
                fin += 1
                ins.then_inc(fin_chain, 1)
                dve.wait_ge(fin_chain, fin)

            def scale_dense(n):
                dve.wait_ge(ffn_ready, n + 1)
                dve.tensor_scalar(y_sb[:, n, :, :], ps_max[:, n % A_RING, :].rearrange("p (t d) -> p t d", d=D),
                                  scale_both[:, 0:1], None, ALU.mult).then_inc(ffn_scaled, 1)

            def finish_att(n):
                rows = LAST_ROWS if n == LAST else 128
                dve.wait_ge(att_loaded[n], 32)
                fin_link(dve.reciprocal(sums[0:rows, n, :], sums[0:rows, n, :]))
                dve.tensor_tensor(att[0:rows, n, :], att[0:rows, n, :], sums[0:rows, n, :], ALU.mult).then_inc(att_ready, 1)

            def finish_last(half):
                _, i, blocks = ENDS[HALVES[half]]
                cols = slice(i * 128, (i + blocks) * 128)
                dve.wait_ge(sums_ready, half + 1)
                fin_link(dve.reciprocal(sums_last[:, cols], (ps_max[:, 0, :], ps_out)[half][:, cols]))
                dve.tensor_tensor(att_last[:, cols], raw_sb[:, 1, cols], sums_last[:, cols], ALU.mult).then_inc(att_ready, 1)

            def add_dense(n):
                dve.wait_ge(ffn_done, n + 1)
                tiles = slice(n * TC, (n + 1) * TC)
                dve.tensor_tensor(y_out[:, n, :, :], xs[:, tiles, :], ffn[:, tiles, :], ALU.add).then_inc(x_ffn_ready[0], 1)

            def finish_out(m):
                n, i, blocks = ENDS[m]
                dve.wait_ge(y_ready, m + 1)
                dve.wait_ge(x_ffn_ready[n // NC], n % NC + 1)
                to = y_out[:, n, i:i + blocks, :]
                dve.tensor_tensor(to, ps[:, END_BANKS[m], 0:blocks * 128].rearrange("p (t d) -> p t d", d=D),
                                  to, ALU.add).then_inc(y_out_ready, 1)

            finish_att(0)
            finish_att(1)
            for n in range(B * NC):
                scale_dense(n)
            finish_att(LAST)
            add_dense(0)
            add_dense(1)
            finish_att(2)
            finish_out(0)
            finish_out(1)
            finish_last(0)
            finish_last(1)
            finish_out(2)
            finish_out(3)
            finish_out(4)

        @block.tensor
        def _(pe):
            def keep_clock(count, bank):
                for _ in range(count):
                    pe.matmul(ps[:, bank, 0:256], max_parts[:, 0, :], max_parts[:].rearrange("p c a -> p (c a)"),
                              start=True, stop=True)

            pe.wait_ge(eps_set, 2)
            keep_clock(KEEP_FIRST, 7)
            pe.wait_ge(consts, 1)
            pe.wait_ge(w_loaded, 48)

            def turn_x(n):
                for i in range(TC):
                    pe.wait_ge(xn_ready, n * TC + i + 1)
                    last = pe.transpose(ps[:, TURN_BANKS[n], i * 128:(i + 1) * 128], xn[:, n * TC + i, :], identf[:])
                last.then_inc(turned, 1)

            def project_in(n, between=lambda: None):
                bq, bk, bv = PREP_BANKS[n]
                pe.wait_ge(xnT_ready, n + 1)
                moving = xnT[:, n * C:(n + 1) * C]
                pe.matmul(ps[:, bq, :], w_qk[:, 0, :], moving, start=True, stop=True).then_inc(q_ready, 1)
                between()
                pe.matmul(ps[:, bk, :], w_qk[:, 1, :], moving, start=True, stop=True).then_inc(k_ready, 1)
                between()
                if n >= NC:
                    pe.wait_ge(v_copied, n)
                for i in range(TC):
                    last = pe.matmul(ps[:, bv, i * 128:(i + 1) * 128], xnT[:, (n * TC + i) * 128:(n * TC + i + 1) * 128],
                                     w_sb[:, 2, :], start=True, stop=True)
                last.then_inc(v_ready, 1)
                between()

            turn_x(0)
            pe.wait_ge(w_turned, 2)
            project_in(0)
            turn_x(1)
            project_in(1)

            def ring_unit(G, s, n):
                unit = RING[n]
                bank = ps_max[:, n % A_RING, :]
                if n == TURN_AT[1] and isinstance(G, int) and G == 0:
                    return
                count = 1 + (RING_ADD if n == len(RING) - 1 else 0)
                if isinstance(G, int) and G == 0 and n == TURN_AT[1] - 1:
                    count += 1
                if isinstance(G, int) and G == NG:
                    count += n
                if unit[0] == TURN:
                    c = unit[1]
                    pe.wait_ge(max_ready, NC * (G - c) + c + 1)
                    pe.wait_ge(bank_free, NR * G + (A_RING if isinstance(G, int) and G == NG else n + 1))
                    pe.transpose(turned_view(bank), max_parts[:, c, :], ident[:]).then_inc(bank_ready, count)
                    return
                c, pieces = unit
                pe.wait_ge(bank_free, NR * G + n + 1)
                for col, j, i, k0, nk, _, _ in pieces:
                    width = nk * 128
                    q0 = (i % TC) * 128
                    last = pe.matmul(bank[:, col:col + width], qr[0:PAD_ROWS, s, i // TC, j, q0:q0 + 128],
                                     kr[0:PAD_ROWS, s, k0 // TC, j, (k0 % TC) * 128:(k0 % TC) * 128 + width],
                                     start=True, stop=True)
                last.then_inc(bank_ready, count)

            def pass_a(G, s, turn, ns):
                for n in ns:
                    if n == 0:
                        pe.wait_ge(rows_loaded[s][0], 16 * (1 + NP) * (turn + 1))
                    if n == C1_FIRST:
                        pe.wait_ge(rows_loaded[s][1], 16 * (1 + NP) * (turn + 1))
                    ring_unit(G, s, n)

            def scores(G, s, n, step):
                c, pieces = STEPS[step]
                if step == 0 or step == Q0_FREE:
                    pe.wait_ge(max_rows[c], 16 * (G + 2))
                if not (isinstance(n, int) and n < S_RING):
                    pe.wait_ge(probs_ready, n + 1 - S_RING)
                for col, j, kb, q0, width, _ in pieces:
                    to = ps_scores[:, step % S_RING, :]
                    last = pe.matmul(to[:, col:col + width],
                                     kr[0:MAX_ROWS, s, kb // TC, j, (kb % TC) * 128:(kb % TC) * 128 + 128],
                                     qr[0:MAX_ROWS, s, c, j, q0:q0 + width], start=True, stop=True)
                last.then_inc(scores_ready, 1)

            def values(G, s, place, between):
                steps = VALUES.get(place)
                if steps is None:
                    between(0)
                    return
                c = STEPS[steps[0]][0]
                between(0)
                if steps[0] == 0:
                    pe.wait_ge(v_slot_ready, G + 1)
                if steps[0] in (0, Q0_FREE):
                    pe.wait_ge(out_free, NC * G + c + 1)
                if steps[-1] in MASKED_STEPS:
                    pe.wait_ge(probs_masked, len(MASKED_STEPS) * G + MASKED_STEPS.index(steps[-1]) + 1)
                else:
                    pe.wait_ge(probs_ready, NSTEP * G + steps[-1] + 1)
                todo = value_pieces(place)
                for m, (step, (col, j, kb, q0, width, _)) in enumerate(todo):
                    ins = pe.matmul(ps_out[32 * j:32 * j + 32, q0:q0 + width], vr[:, s, kb, j, :],
                                    probs[:, step % P_RING, col:col + width], start=(kb == 0), stop=(kb == TC * c + 2),
                                    skip_group_check=True)
                    if m == len(todo) - 1:
                        if steps[-1] in (Q0_FREE - 1, NSTEP - 1):
                            ins.then_inc(out_ready, 1)
                        else:
                            ins.then_inc(probs_free, len(steps))
                    between(m + 1)

            def group(G, s, turn, following=True, after_next=True, extra=None):
                for place in range(FIRST, NSTEP + FIRST):
                    if place < NSTEP:
                        scores(G, s, NSTEP * G + place, place)
                    elif following:
                        scores(G + 1, 1 - s, NSTEP * (G + 1) + place - NSTEP, place - NSTEP)
                    elif place >= NSTEP + 2:
                        break

                    def between(m):
                        if place < NSTEP + A_FIRST:
                            if following:
                                pass_a(G + 1, 1 - s, turn + s, SPREAD.get((place, m), []))
                        elif after_next:
                            pass_a(G + 2, s, turn + 1, SPREAD.get((place - NSTEP, m), []))
                        elif following and TURN_AT[1] in SPREAD.get((place - NSTEP, m), []):
                            ring_unit(NG, s, TURN_AT[1])

                    if place < NSTEP + 2:
                        values(G, s, place, between)
                    else:
                        values(G + 1, 1 - s, place - NSTEP, between)
                    if extra:
                        extra(place)

            pe.wait_ge(v_copied, 1)
            pe.wait_ge(rest_ready, 2)
            turn_x(2)
            ahead = iter(range(AHEAD))

            def more_a(count=1):
                for _ in range(count):
                    pass_a(0, 0, 0, [next(ahead)])

            more_a(A_BEFORE[0])
            keep_clock(KEEP_LATE, 3)
            turn_x(3)
            more_a(A_BEFORE[1])
            pe.wait_ge(v_copied, NC)
            pe.wait_ge(rest_ready, 2 * NC)
            project_in(2, more_a)
            more_a(A_BEFORE[2])
            pe.wait_ge(xnT_ready, B * NC)
            project_in(3, more_a)
            for n in ahead:
                pass_a(0, 0, 0, [n])
            pe.wait_ge(v_copied, B * NC - 1)
            rest = [(0, n) for n in range(AHEAD, len(RING))] + [
                (1, n) for n in sorted(n for (place, _), ns in SPREAD.items() if place < FIRST for n in ns)]

            def rest_of_a(place, m):
                if m == 0:
                    for G, n in rest[len(rest) * place // FIRST:len(rest) * (place + 1) // FIRST]:
                        pass_a(G, G, 0, [n])

            for place in range(FIRST):
                scores(0, 0, place, place)
                if place == 0:
                    pe.wait_ge(v_copied, B * NC)
                values(0, 0, place, lambda m: rest_of_a(place, m))
            with pe.Fori(0, NLOOP) as it:
                for s in range(2):
                    group(2 * it + s, s, it)
            group(NG - 2, 0, NG // 2 - 1, after_next=False)

            def dense(n):
                if n == 0:
                    pe.wait_ge(bank_free, NR * NG + A_RING + TURN_AT[1] + 1)
                    pe.wait_ge(quantised, 1)
                if n >= A_RING:
                    pe.wait_ge(ffn_scaled, n - A_RING + 1)
                for i in range(TC):
                    t = n * TC + i
                    last = pe.matmul(ps_max[:, n % A_RING, i * 128:(i + 1) * 128], xq[:, t * 128:(t + 1) * 128], kq[:],
                                     start=True, stop=True)
                last.then_inc(ffn_ready, 1)

            def project(m):
                n, i, blocks = ENDS[m]
                pe.wait_ge(att_ready, ATT_ORDER[m])
                if m == 2:
                    pe.wait_ge(probs_ready, NSTEP * NG)
                if m == 0:
                    pe.wait_ge(f_loaded, 16 * 5)
                    pe.wait_ge(ffn_scaled, B * NC)
                for k in range(blocks):
                    cols = slice((i + k) * 128, (i + k + 1) * 128)
                    to = ps[:, END_BANKS[m], k * 128:(k + 1) * 128]
                    if n == LAST:
                        pe.matmul(to, att[0:LAST_ROWS, n, cols], w_sb[0:LAST_ROWS, 3, :], start=True, stop=False)
                        last = pe.matmul(to, att_last[:, cols], wo_last[:], start=False, stop=True)
                    else:
                        last = pe.matmul(to, att[:, n, cols], w_sb[:, 3, :], start=True, stop=True)
                last.then_inc(y_ready, 1)

            def spread_sums(half):
                _, i, blocks = ENDS[HALVES[half]]
                cols = slice(i * 128, (i + blocks) * 128)
                if half == 0:
                    pe.wait_ge(last_set, 3)
                    pe.wait_ge(wo_loaded, 16 * J)
                    pe.wait_ge(out_free, NC * NG + 1)
                pe.matmul((ps_max[:, 0, :], ps_out)[half][:, cols], spread[:], raw_sb[:, 1, cols],
                          start=True, stop=True).then_inc(sums_ready, 1)

            def last_group_extra(place):
                if place in DENSE_PLACES:
                    dense(DENSE_PLACES.index(place))
                if place == NSTEP - 1:
                    project(0)

            group(NG - 1, 1, NG // 2 - 1, following=False, after_next=False, extra=last_group_extra)
            project(1)
            spread_sums(0)
            spread_sums(1)
            project(2)
            project(3)
            project(4)


_INS = ['L0_attn_x', 'L0_attn_WQ', 'L0_attn_WK', 'L0_attn_WV', 'L0_attn_WO', 'L0_ffn_kernel',
        'L0_ffn_input_scale', 'L0_ffn_kernel_scale', 'L0_ffn_bias']


def kernel(**inputs):
    import numpy as _np
    import concourse.bacc as _bacc
    from concourse import mybir as _mybir
    from concourse.bass_utils import run_bass_kernel_spmd as _run

    nc = _bacc.Bacc("TRN2", target_bir_lowering=False, num_devices=1)
    arrays, args = {}, []
    for name in _INS:
        a = _np.ascontiguousarray(inputs[name])
        arrays[f"in_{name}"] = a
        args.append(nc.dram_tensor(f"in_{name}", a.shape, _mybir.dt.from_np(a.dtype), kind="ExternalInput").ap())
    out = nc.dram_tensor("out", (B, S, D), fp32, kind="ExternalOutput").ap()
    attention_kernel(nc, *args, out)
    r = _run(nc, [arrays], core_ids=[0])
    return r.results[0]["out"]
```
